# Optimizing a Trainium2 kernel written in Bass

```python
import numpy as np
import jax
import jax.numpy as jnp

def _softmax(x, axis=-1):
    return jax.nn.softmax(x, axis=axis)

def _gelu(x):
    return jax.nn.gelu(x, approximate=True)

def _silu(x):
    return jax.nn.silu(x)

def _sigmoid(x):
    return jax.nn.sigmoid(x)

def _layernorm(x, axis=-1, eps=1e-05):
    m = jnp.mean(x, axis=axis, keepdims=True)
    v = jnp.var(x, axis=axis, keepdims=True)
    return (x - m) / jnp.sqrt(v + eps)

def _scatter_add(tgt, idx, src, axis=0):
    return tgt.at[idx].add(src)

def _segment_sum(src, seg, n):
    return jax.ops.segment_sum(src, seg, n)
kernel_name = 'mk_early_fusion_embed_d1_tok_img512_r4_e080c5'

def setup_inputs(seed: int=0):
    np.random.seed(seed)
    _w = jnp.asarray

    def _rec_inputs():
        import jax
        import jax.numpy as jnp
        _rk = jax.random.key(seed)
        x = -0.000477451 + 1.00034 * jax.random.normal(jax.random.fold_in(_rk, 1), (16, 32, 32, 29), jnp.float32)
        x_txt = jax.random.randint(jax.random.fold_in(_rk, 51), (16, 77), 0, 10000, jnp.int32)
        return (x, x_txt)
    x, x_txt = _rec_inputs()

    def _L0_tok_setup():
        import jax, jax.numpy as jnp
        import numpy as np
        import math
        H, W_DIM, D_MODEL, B = (32, 32, 128, 128)
        F_TOTAL = 29
        SEQ_LEN = H * W_DIM

        def make_pe(seq_len: int, d_model: int) -> jnp.ndarray:
            position = np.arange(seq_len, dtype=np.float32)[:, None]
            div_term = np.exp(np.arange(0, d_model, 2, dtype=np.float32) * (-math.log(10000.0) / d_model))
            pe = np.zeros((seq_len, d_model), dtype=np.float32)
            pe[:, 0::2] = np.sin(position * div_term)
            pe[:, 1::2] = np.cos(position * div_term)
            return jnp.asarray(pe)
        key = jax.random.key(seed)
        k1, k2 = jax.random.split(key)
        state_tensor = jax.random.normal(k1, (B, H, W_DIM, F_TOTAL), dtype=jnp.float32)
        W = jax.random.normal(k2, (F_TOTAL, D_MODEL), dtype=jnp.float32) * 0.05
        return {'state_tensor': state_tensor, 'W': W}
    _L0_tok_all = _L0_tok_setup()
    _L0_tok_in = {k: v for k, v in _L0_tok_all.items() if k in ('W',)}
    del _L0_tok_all

    def _L0_txt_setup():
        import jax, jax.numpy as jnp
        import numpy as np
        B, S, H = (64, 512, 128)
        VOCAB = 10000

        def _syntax_info(token_ids):
            t = token_ids
            opens = (t == 40) | (t == 123) | (t == 91)
            closes = (t == 41) | (t == 125) | (t == 93)
            delta = opens.astype(jnp.int32) - closes.astype(jnp.int32)
            s = jnp.cumsum(delta, axis=1)
            run_min = jax.lax.cummin(s, axis=1)
            nesting = jnp.clip(s - jnp.minimum(run_min, 0), 0, 15)
            segments = jnp.cumsum((t > 39990).astype(jnp.int32), axis=1) % 8
            return (nesting, segments)
        key = jax.random.key(seed)
        k1, k2, k3, k4, k5 = jax.random.split(key, 5)
        token_ids = jax.random.randint(k1, (B, S), 0, VOCAB, dtype=jnp.int64) if jax.config.jax_enable_x64 else jax.random.randint(k1, (B, S), 0, VOCAB, dtype=jnp.int32)
        std = 0.02
        pos_table = jax.random.normal(k2, (S, H), dtype=jnp.float32) * std
        nest_table = jax.random.normal(k3, (16, H), dtype=jnp.float32) * std
        seg_table = jax.random.normal(k4, (8, H), dtype=jnp.float32) * std
        W = jax.random.normal(k5, (3 * H, H), dtype=jnp.float32) * (1.0 / np.sqrt(3 * H))
        return {'token_ids': token_ids, 'pos_table': pos_table, 'nest_table': nest_table, 'seg_table': seg_table, 'W': W}
    _L0_txt_all = _L0_txt_setup()
    _L0_txt_in = {k: v for k, v in _L0_txt_all.items() if k in ('pos_table', 'nest_table', 'seg_table', 'W')}
    del _L0_txt_all

    def _L0_attn_setup():
        import jax, jax.numpy as jnp
        import numpy as np
        INNER_DIM = 64
        HEAD_NUM = 8
        D_MODEL = 128
        key = jax.random.key(seed)
        k1, k2, k3 = jax.random.split(key, 3)
        x = jax.random.normal(k1, (4, 512, D_MODEL), dtype=jnp.float32)
        kernel = jax.random.uniform(k2, (3 * HEAD_NUM, D_MODEL, INNER_DIM), dtype=jnp.float32, minval=-0.05, maxval=0.05)
        head_kernel = jax.random.uniform(k3, (INNER_DIM * HEAD_NUM, D_MODEL), dtype=jnp.float32, minval=-0.05, maxval=0.05)
        return {'x': x, 'kernel': kernel, 'head_kernel': head_kernel}
    _L0_attn_all = _L0_attn_setup()
    _L0_attn_in = {k: v for k, v in _L0_attn_all.items() if k in ('kernel', 'head_kernel')}
    del _L0_attn_all

    def _L0_ffn_setup():
        import jax, jax.numpy as jnp
        import numpy as np
        B, T, C = (8, 256, 128)
        H = 256
        G, EG = (2, 4)
        E = G * EG
        K = 2
        LN_EPS = 1e-05

        def _swiglu(x):
            a, b = jnp.split(x, 2, axis=-1)
            return jax.nn.silu(a) * b
        key = jax.random.key(seed)
        ks = jax.random.split(key, 8)
        n = lambda k, shape, s: jax.random.normal(k, shape, dtype=jnp.float32) * s
        return {'x': n(ks[0], (B, T, C), 1.0), 'ln_scale': jnp.ones((C,), jnp.float32), 'ln_bias': jnp.zeros((C,), jnp.float32), 'shared_in_w': n(ks[1], (2 * H, C), 0.02), 'shared_out_w': n(ks[2], (C, H), 0.02), 'shared_out_b': jnp.zeros((C,), jnp.float32), 'expert_in_w': n(ks[3], (2 * H, C), 0.02), 'expert_out_weight': n(ks[4], (E, C, H), 0.02), 'expert_out_bias': jnp.zeros((E, C), jnp.float32), 'group_gate_w': n(ks[5], (G, C), 0.02), 'expert_gate_w': n(ks[6], (E, C), 0.02), 'group_bias': jnp.zeros((G,), jnp.float32), 'expert_bias': jnp.zeros((E,), jnp.float32)}
    _L0_ffn_all = _L0_ffn_setup()
    _L0_ffn_in = {k: v for k, v in _L0_ffn_all.items() if k in ('ln_scale', 'ln_bias', 'shared_in_w', 'shared_out_w', 'shared_out_b', 'expert_in_w', 'expert_out_weight', 'expert_out_bias', 'group_gate_w', 'expert_gate_w', 'group_bias', 'expert_bias')}
    del _L0_ffn_all
    return {'x': x, 'x_txt': x_txt, 'L0_tok_W': _L0_tok_in['W'], 'L0_txt_pos_table': _L0_txt_in['pos_table'], 'L0_txt_nest_table': _L0_txt_in['nest_table'], 'L0_txt_seg_table': _L0_txt_in['seg_table'], 'L0_txt_W': _L0_txt_in['W'], 'L0_attn_kernel': _L0_attn_in['kernel'], 'L0_attn_head_kernel': _L0_attn_in['head_kernel'], 'L0_ffn_ln_scale': _L0_ffn_in['ln_scale'], 'L0_ffn_ln_bias': _L0_ffn_in['ln_bias'], 'L0_ffn_shared_in_w': _L0_ffn_in['shared_in_w'], 'L0_ffn_shared_out_w': _L0_ffn_in['shared_out_w'], 'L0_ffn_shared_out_b': _L0_ffn_in['shared_out_b'], 'L0_ffn_expert_in_w': _L0_ffn_in['expert_in_w'], 'L0_ffn_expert_out_weight': _L0_ffn_in['expert_out_weight'], 'L0_ffn_expert_out_bias': _L0_ffn_in['expert_out_bias'], 'L0_ffn_group_gate_w': _L0_ffn_in['group_gate_w'], 'L0_ffn_expert_gate_w': _L0_ffn_in['expert_gate_w'], 'L0_ffn_group_bias': _L0_ffn_in['group_bias'], 'L0_ffn_expert_bias': _L0_ffn_in['expert_bias']}

def reference(x, x_txt, L0_tok_W, L0_txt_pos_table, L0_txt_nest_table, L0_txt_seg_table, L0_txt_W, L0_attn_kernel, L0_attn_head_kernel, L0_ffn_ln_scale, L0_ffn_ln_bias, L0_ffn_shared_in_w, L0_ffn_shared_out_w, L0_ffn_shared_out_b, L0_ffn_expert_in_w, L0_ffn_expert_out_weight, L0_ffn_expert_out_bias, L0_ffn_group_gate_w, L0_ffn_expert_gate_w, L0_ffn_group_bias, L0_ffn_expert_bias):
    import jax
    import jax.numpy as jnp

    def _L0_tok_ref(state_tensor, W):
        import jax, jax.numpy as jnp
        import numpy as np
        import math
        H, W_DIM, D_MODEL, B = (32, 32, 128, 128)
        F_TOTAL = 29
        SEQ_LEN = H * W_DIM

        def make_pe(seq_len: int, d_model: int) -> jnp.ndarray:
            position = np.arange(seq_len, dtype=np.float32)[:, None]
            div_term = np.exp(np.arange(0, d_model, 2, dtype=np.float32) * (-math.log(10000.0) / d_model))
            pe = np.zeros((seq_len, d_model), dtype=np.float32)
            pe[:, 0::2] = np.sin(position * div_term)
            pe[:, 1::2] = np.cos(position * div_term)
            return jnp.asarray(pe)
        b, h, w, f = state_tensor.shape
        s = h * w
        x = state_tensor.reshape(b, s, f)
        emb = jnp.einsum('bsf,fd->bsd', x, W)
        pe = make_pe(s * 2, W.shape[1])[:s]
        return emb + pe[None, :, :]

    def _L0_txt_ref(token_ids, pos_table, nest_table, seg_table, W):
        import jax, jax.numpy as jnp
        import numpy as np
        B, S, H = (64, 512, 128)
        VOCAB = 10000

        def _syntax_info(token_ids):
            t = token_ids
            opens = (t == 40) | (t == 123) | (t == 91)
            closes = (t == 41) | (t == 125) | (t == 93)
            delta = opens.astype(jnp.int32) - closes.astype(jnp.int32)
            s = jnp.cumsum(delta, axis=1)
            run_min = jax.lax.cummin(s, axis=1)
            nesting = jnp.clip(s - jnp.minimum(run_min, 0), 0, 15)
            segments = jnp.cumsum((t > 39990).astype(jnp.int32), axis=1) % 8
            return (nesting, segments)
        b, s = token_ids.shape
        positions = jnp.arange(s)
        pos_emb = jnp.broadcast_to(pos_table[positions][None], (b, s, pos_table.shape[-1]))
        nesting, segments = _syntax_info(token_ids)
        nest_emb = nest_table[nesting]
        seg_emb = seg_table[segments]
        combined = jnp.concatenate([pos_emb, nest_emb, seg_emb], axis=-1)
        return jnp.einsum('bsk,kh->bsh', combined, W)

    def _L0_attn_ref(x, kernel, head_kernel):
        import jax, jax.numpy as jnp
        import numpy as np
        INNER_DIM = 64
        HEAD_NUM = 8
        D_MODEL = 128
        H, K = (HEAD_NUM, INNER_DIM)
        w = kernel.reshape(H, 3, kernel.shape[1], K)
        wq, wk, wv = (w[:, 0], w[:, 1], w[:, 2])
        q = jnp.einsum('bsd,hdk->bhsk', x, wq)
        k = jnp.einsum('bsd,hdk->bhsk', x, wk)
        v = jnp.einsum('bsd,hdk->bhsk', x, wv)
        scores = jnp.einsum('bhsk,bhtk->bhst', q, k) / jnp.sqrt(jnp.asarray(K, x.dtype))
        probs = jax.nn.softmax(scores, axis=-1)
        o = jnp.einsum('bhst,bhtk->bhsk', probs, v)
        B, _, S, _ = o.shape
        concated = jnp.transpose(o, (0, 2, 1, 3)).reshape(B, S, H * K)
        return jnp.einsum('bse,ed->bsd', concated, head_kernel)

    def _L0_ffn_ref(x, ln_scale, ln_bias, shared_in_w, shared_out_w, shared_out_b, expert_in_w, expert_out_weight, expert_out_bias, group_gate_w, expert_gate_w, group_bias, expert_bias):
        import jax, jax.numpy as jnp
        import numpy as np
        B, T, C = (8, 256, 128)
        H = 256
        G, EG = (2, 4)
        E = G * EG
        K = 2
        LN_EPS = 1e-05

        def _swiglu(x):
            a, b = jnp.split(x, 2, axis=-1)
            return jax.nn.silu(a) * b
        Bx, Tx, Cx = x.shape
        S = Bx * Tx
        flat = x.reshape(S, Cx)
        mu = flat.mean(-1, keepdims=True)
        var = ((flat - mu) ** 2).mean(-1, keepdims=True)
        flat = (flat - mu) * jax.lax.rsqrt(var + LN_EPS) * ln_scale + ln_bias
        h_shared = _swiglu(flat @ shared_in_w.T)
        out_shared = h_shared @ shared_out_w.T + shared_out_b
        g_logits = flat @ group_gate_w.T + group_bias
        g_idx = jnp.argmax(g_logits, axis=-1)
        e_logits = (flat @ expert_gate_w.T).reshape(S, G, EG)
        e_sel = jnp.take_along_axis(e_logits, g_idx[:, None, None], axis=1)[:, 0, :]
        e_sel = e_sel + expert_bias.reshape(G, EG)[g_idx]
        e_probs = jax.nn.softmax(e_sel, axis=-1)
        topv, topi = jax.lax.top_k(e_probs, K)
        topv = topv / (topv.sum(-1, keepdims=True) + 1e-08)
        disp = g_idx[:, None] * EG + topi
        h_expert = _swiglu(flat @ expert_in_w.T)
        rows = jnp.arange(S)[:, None]
        comb = jnp.zeros((S, E), flat.dtype).at[rows, disp].add(topv)
        cnt = jnp.zeros((S, E), flat.dtype).at[rows, disp].add(1.0)
        routed = cnt @ expert_out_bias
        for e in range(E):
            routed = routed + comb[:, e:e + 1] * (h_expert @ expert_out_weight[e].T)
        return (out_shared + routed).reshape(Bx, Tx, Cx)
    h = _L0_tok_ref(x, L0_tok_W)
    h = jnp.concatenate([h, _L0_txt_ref(x_txt, L0_txt_pos_table, L0_txt_nest_table, L0_txt_seg_table, L0_txt_W)], axis=1)
    h = h + _L0_attn_ref(_layernorm(h, axis=-1), L0_attn_kernel, L0_attn_head_kernel)
    h = h + _L0_ffn_ref(_layernorm(h, axis=-1), L0_ffn_ln_scale, L0_ffn_ln_bias, L0_ffn_shared_in_w, L0_ffn_shared_out_w, L0_ffn_shared_out_b, L0_ffn_expert_in_w, L0_ffn_expert_out_weight, L0_ffn_expert_out_bias, L0_ffn_group_gate_w, L0_ffn_expert_gate_w, L0_ffn_group_bias, L0_ffn_expert_bias)
    return h

_drawn_inputs = setup_inputs


def setup_inputs(seed=0):
    import zlib

    import numpy as np

    out = dict(_drawn_inputs(seed))
    spreads = {'L0_ffn_ln_scale': (1.0, 0.2),
     'L0_ffn_ln_bias': (0.0, 0.1),
     'L0_ffn_shared_out_b': (0.0, 0.1),
     'L0_ffn_expert_out_bias': (0.0, 0.1),
     'L0_ffn_group_bias': (0.0, 0.1),
     'L0_ffn_expert_bias': (0.0, 0.1)}
    factors = {'L0_txt_pos_table': 5.416,
     'L0_txt_seg_table': 2.795,
     'L0_ffn_shared_in_w': 4.762,
     'L0_ffn_shared_out_w': 4.58,
     'L0_ffn_expert_in_w': 6.723,
     'L0_ffn_expert_out_weight': 6.951}
    for name, (base, spread) in spreads.items():
        noise = np.random.default_rng([zlib.crc32(name.encode()), seed]).standard_normal(out[name].shape)
        drawn = base * np.exp(spread * noise) if base else spread * noise
        out[name] = jnp.asarray(drawn.astype(out[name].dtype))
    for name, factor in factors.items():
        out[name] = (out[name] * factor).astype(out[name].dtype)
    return out
```

```python
from contextlib import ExitStack

import numpy as np

import concourse.bass as bass
from concourse import mybir
from concourse.alu_op_type import AluOpType as ALU

F32 = mybir.dt.float32
F32R = mybir.dt.float32r
I32 = mybir.dt.int32
ACT = mybir.ActivationFunctionType
AX = mybir.AxisListType

P = 128
B, HW, F = 16, 1024, 29
TXT = 77
T = HW + TXT
TP = T + 1
IMG = HW // P
NT = IMG + 1
TW = NT * P
D = 128
H, DH = 8, 64
PAIRS = H // 2
CHUNK = 368
CHUNKS = [(0, CHUNK), (CHUNK, CHUNK), (2 * CHUNK, TP - 2 * CHUNK)]
NC = len(CHUNKS)
STEPS = NC * NT
ALL = PAIRS * STEPS
GW = 3 * P
E, EG, HID = 8, 4, 256
KC = HID // P
EPS = 1e-5
NEST, SEG = 16, 8
LANES = 3
NP = 2


def rows(t):
    return P if t < IMG else TXT


def queries(j):
    return P if j < IMG else TP - IMG * P


def plan(attn, post, prep):
    at = [[] for _ in range(ALL)]
    if attn:
        for q in range(PAIRS * NC - 1):
            at[NT * (q + 1) + 2].append(("sum", q))
        for j in range(NT):
            at[j].append(("v", j))
    if post:
        at[1].append(("sum", PAIRS * NC - 1))
        for g in range(3):
            at[5 + g].append(("proj", g))
            at[15 + g].append(("turn2", g))
        at[19].append(("gate",))
        at[24].append(("count",))
        units = []
        for c in range(3):
            units += [("up", c, path, k, half) for path in range(2) for k in range(KC) for half in range(2)]
            units += [("pause",)] * 2
            units += [("shared", c)] + [("expert", 3 * c + j, g) for j in range(3) for g in range(2)]
        first, last = 25, 78
        for n, u in enumerate(units):
            if u != ("pause",):
                at[first + n * (last - first) // len(units)].append(u)
    if prep:
        at[56].append(("turnx",))
        at[57].append(("embed", 0))
        at[58].append(("embed", 1))
        for g in range(3):
            at[68 + g].append(("turn1", g))
    for p in range(PAIRS):
        if (attn and p < PAIRS - 1) or (prep and p == PAIRS - 1):
            nxt = (p + 1) % PAIRS
            qk = [("qk", nxt, what, c) for what in ("k", "q") for c in range(NC)]
            for n, u in enumerate(qk):
                at[STEPS * p + n // 2].append(u)
            mx = [("max", nxt, i, j, c) for i in range(2) for j in range(NT) for c in range(NC)]
            first, last = 3, 24
            for n, u in enumerate(mx):
                at[STEPS * p + first + n * (last - first) // len(mx)].append(u)
            at[STEPS * p + 25].append(("maxrow", nxt))
    return at


class Segment:

    def __init__(self, attn, post, prep, before):
        self.attn, self.post, self.prep = attn, post, prep
        self.at = plan(attn, post, prep)
        self.before = before
        self.uses = [0] * LANES
        self.bank, self.order = {}, {}
        n = 0
        for units in self.at:
            for u in units:
                k = n % LANES
                self.bank[u] = k
                self.uses[k] += 1
                self.order[u] = self.uses[k]
                n += 1

    def after(self, times):
        return [b + times * u for b, u in zip(self.before, self.uses)]

    def value(self, it, u):
        k = self.bank[u]
        return it * self.uses[k] + self.before[k] + self.order[u]


def fusion_kernel(nc, x, x_txt, tok_w, pos, nest, seg, txt_w, attn_w, head_w, ln_scale, ln_bias,
                  sh_in, sh_out, sh_out_b, ex_in, ex_out, ex_out_b, group_w, expert_w,
                  group_b, expert_b, pe_table, out):
    ctx = ExitStack()
    text_dram = nc.dram_tensor("text_rows", (B, TXT, D), F32, kind="Internal").ap()
    resid_dram = nc.dram_tensor("resid_rows", (B, P, NT * D), F32, kind="Internal").ap()

    def sb(stack, name, shape, dt=F32):
        return stack.enter_context(nc.sbuf_tensor(name, shape, dt))

    def sem(name):
        return ctx.enter_context(nc.semaphore(name))

    scores = ctx.enter_context(nc.psum_tensor("scores", [P, 2, 2, 512], F32))
    o_ps = ctx.enter_context(nc.psum_tensor("o_ps", [P, 512], F32))
    work = ctx.enter_context(nc.psum_tensor("work", [P, LANES, 512], F32))

    ident = sb(ctx, "ident", [P, P])
    ones = sb(ctx, "ones", [P, DH])
    wqk_hi = sb(ctx, "wqk_hi", [P, 2, H, DH], F32R)
    wqk_lo = sb(ctx, "wqk_lo", [P, 2, H, DH], F32R)
    wv_hi = sb(ctx, "wv_hi", [P, H * DH], F32R)
    wv_lo = sb(ctx, "wv_lo", [P, H * DH], F32R)
    wo = sb(ctx, "wo", [P, PAIRS, D])
    up_hi = sb(ctx, "up_hi", [P, 2, 4, P], F32R)
    up_lo = sb(ctx, "up_lo", [P, 2, 4, P], F32R)
    down_hi = sb(ctx, "down_hi", [P, KC, E * D], F32R)
    down_lo = sb(ctx, "down_lo", [P, KC, E * D], F32R)
    down_sh = sb(ctx, "down_sh", [P, KC, D])
    gate_w = sb(ctx, "gate_w", [P, 2 + E])
    gate_b = sb(ctx, "gate_b", [P, 2 + E])
    ln_cols = sb(ctx, "ln_cols", [P, 2])
    bias_rows = sb(ctx, "bias_rows", [P, 4, D])
    tok_blocks = sb(ctx, "tok_blocks", [P, 4, D])

    loaded = sem("loaded")
    zeroed = sem("zeroed")
    raw_loaded = sem("raw_loaded")
    s_pool = sem("s_pool")
    s_turned = sem("s_turned")
    s_taken = sem("s_taken")
    s_dve = sem("s_dve")
    s_text = sem("s_text")
    s_hi = sem("s_hi")
    s_stored = sem("s_stored")
    s_chain = sem("s_chain")

    with ExitStack() as tmp:
        attn_raw = sb(tmp, "attn_raw", [P, 3 * H, DH])
        in_raw = sb(tmp, "in_raw", [P, 2, 4, D])
        out_raw = sb(tmp, "out_raw", [P, 1 + E, HID])
        gates_raw = sb(tmp, "gates_raw", [2 + E, D])
        pos_raw = sb(tmp, "pos_raw", [TXT, D])
        tab_raw = sb(tmp, "tab_raw", [NEST + SEG, D])
        txt_wr = sb(tmp, "txt_wr", [P, 3, D])
        turned = sb(tmp, "turned", [P, 4, 512])
        tabs_n = sb(tmp, "tabs_n", [P, NEST + SEG])
        tabs_s = sb(tmp, "tabs_s", [P, NEST + SEG])
        pos_t = sb(tmp, "pos_t", [P, TXT])
        base = sb(tmp, "base", [TXT, D])
        rows24 = sb(tmp, "rows24", [NEST + SEG, D])
        tok_i = sb(tmp, "tok_i", [B, TXT], I32)
        tok = sb(tmp, "tok", [B, TXT])
        opens = sb(tmp, "opens", [B, TXT])
        closes = sb(tmp, "closes", [B, TXT])
        one_b = sb(tmp, "one_b", [B, TXT])
        runs = sb(tmp, "runs", [B, TXT])
        low = sb(tmp, "low", [B, TXT])
        idx = sb(tmp, "idx", [B, 2, TXT])
        idx_t = sb(tmp, "idx_t", [TXT, 2, B])
        iota_e = sb(tmp, "iota_e", [TXT, NEST])
        onehot = sb(tmp, "onehot", [TXT, B, NEST + SEG])
        hot_t = sb(tmp, "hot_t", [NEST + SEG, B, TXT])
        text_h = sb(tmp, "text_h", [TXT, B, D])
        block = tmp.enter_context(nc.Block())

        N_ZEROED = 4

        @block.gpsimd
        def _(pool):
            nc.gpsimd.memset(ident[:], 0.0).then_inc(s_pool, 1)
            pool.wait_ge(s_pool, 1)
            nc.gpsimd.affine_select(out=ident[:], in_=ident[:], compare_op=ALU.not_equal, fill=1.0,
                                    base=0, pattern=[[-1, P]], channel_multiplier=1).then_inc(s_pool, 1)
            nc.gpsimd.iota(iota_e[:], pattern=[[1, NEST]], base=0, channel_multiplier=0,
                           allow_small_or_imprecise_dtypes=True).then_inc(s_pool, 1)

        @block.sync
        def _(sp):
            sp.dma_start(tok_i[:], x_txt).then_inc(loaded, 16)
            sp.dma_start(pos_raw[:], pos[0:TXT, :]).then_inc(raw_loaded, 16)
            sp.dma_start(tab_raw[0:NEST, :], nest).then_inc(raw_loaded, 16)
            sp.dma_start(tab_raw[NEST:NEST + SEG, :], seg).then_inc(raw_loaded, 16)
            sp.dma_start(txt_wr[:], txt_w.rearrange("(a p) n -> p a n", p=P)).then_inc(raw_loaded, 16)
            sp.dma_start(gates_raw[0:2, :], group_w).then_inc(raw_loaded, 16)
            sp.dma_start(gates_raw[2:2 + E, :], expert_w).then_inc(raw_loaded, 16)
            sp.dma_start(in_raw[:, 0], sh_in.rearrange("(a p) n -> p a n", p=P)).then_inc(raw_loaded, 16)
            sp.dma_start(in_raw[:, 1], ex_in.rearrange("(a p) n -> p a n", p=P)).then_inc(raw_loaded, 16)
            sp.dma_start(out_raw[:, 0], sh_out).then_inc(raw_loaded, 16)
            sp.dma_start(out_raw[:, 1:], ex_out.rearrange("e p n -> p e n")).then_inc(raw_loaded, 16)
            sp.dma_start(attn_raw[:], attn_w.rearrange("a p n -> p a n")).then_inc(raw_loaded, 16)
            sp.dma_start(wo[:], head_w.rearrange("(a p) n -> p a n", p=P)).then_inc(raw_loaded, 16)
            sp.dma_start(ln_cols[:, 0:1], ln_scale.rearrange("(p a) -> p a", a=1)).then_inc(raw_loaded, 16)
            sp.dma_start(ln_cols[:, 1:2], ln_bias.rearrange("(p a) -> p a", a=1)).then_inc(raw_loaded, 16)
            sp.dma_start(gate_b[:, 0:2], group_b.rearrange("(a n) -> a n", a=1).broadcast_to((P, 2))).then_inc(raw_loaded, 16)
            sp.dma_start(gate_b[:, 2:2 + E], expert_b.rearrange("(a n) -> a n", a=1).broadcast_to((P, E))).then_inc(raw_loaded, 16)
            sp.wait_ge(zeroed, N_ZEROED)
            for q in range(4):
                sp.dma_start(bias_rows[32 * q:32 * q + E, q, :], ex_out_b).then_inc(raw_loaded, 16)
                sp.dma_start(bias_rows[32 * q + E:32 * q + E + 1, q, :],
                             sh_out_b.rearrange("(a n) -> a n", a=1)).then_inc(raw_loaded, 16)
                sp.dma_start(tok_blocks[32 * q:32 * q + F, q, :], tok_w).then_inc(raw_loaded, 16)
            sp.wait_ge(s_text, 1)
            sp.dma_start(text_dram.rearrange("b t d -> t b d"), text_h[:]).then_inc(s_stored, 16)
            sp.wait_ge(s_stored, 16)
            sp.wait_ge(raw_loaded, 16 * 28)

        in_turns = [(in_raw[:, w, a, :], P) for w in range(2) for a in range(4)]
        out_turns = [(out_raw[:, e, k * P:(k + 1) * P], P) for e in range(1 + E) for k in range(KC)]
        turns = in_turns + out_turns
        groups = [turns[n:n + 4] for n in range(0, len(turns), 4)]
        NG = len(groups)

        @block.tensor
        def _(pe):
            pe.wait_ge(raw_loaded, 16 * 28)
            pe.wait_ge(s_pool, 2)
            nc.tensor.transpose(work[:, 0, 0:2 + E], gates_raw[:], ident[0:2 + E, 0:2 + E])
            nc.tensor.transpose(work[:, 0, 16:16 + TXT], pos_raw[:], ident[0:TXT, 0:TXT])
            nc.tensor.transpose(work[:, 0, 128:128 + NEST + SEG], tab_raw[:],
                                ident[0:NEST + SEG, 0:NEST + SEG]).then_inc(s_turned, 1)
            pe.wait_ge(s_dve, 1)
            nc.tensor.transpose(work[0:TXT, 1, 0:B], idx[:, 0, :], ident[0:B, 0:B])
            nc.tensor.transpose(work[0:TXT, 1, B:2 * B], idx[:, 1, :], ident[0:B, 0:B]).then_inc(s_turned, 1)
            pe.wait_ge(s_taken, 1)
            nc.tensor.matmul(work[0:TXT, 2, 0:D], pos_t[:], txt_wr[:, 0, :], start=True, stop=True)
            nc.tensor.matmul(work[0:NEST + SEG, 2, D:2 * D], tabs_n[:], txt_wr[:, 1, :], start=True, stop=False)
            nc.tensor.matmul(work[0:NEST + SEG, 2, D:2 * D], tabs_s[:], txt_wr[:, 2, :],
                             start=False, stop=True).then_inc(s_turned, 1)
            pe.wait_ge(s_taken, 3)
            for g in range(4):
                for i in range(4):
                    last = nc.tensor.transpose(scores[0:NEST + SEG, g // 2, g % 2, i * TXT:(i + 1) * TXT],
                                               onehot[:, 4 * g + i, :], ident[0:TXT, 0:TXT])
                last.then_inc(s_turned, 1)
            for g in range(4):
                pe.wait_ge(s_taken, 4 + g)
                for i in range(4):
                    last = nc.tensor.matmul(scores[0:TXT, g // 2, g % 2, i * D:(i + 1) * D],
                                            hot_t[:, 4 * g + i, :], rows24[:], start=True, stop=True)
                last.then_inc(s_turned, 1)
            for g, group in enumerate(groups):
                if g >= LANES:
                    pe.wait_ge(s_taken, 8 + g - LANES)
                for i, (src, _) in enumerate(group):
                    last = nc.tensor.transpose(work[:, g % LANES, i * P:(i + 1) * P], src, ident[:])
                last.then_inc(s_turned, 1)

        @block.scalar
        def _(act):
            act.wait_ge(raw_loaded, 16 * 28)
            v = attn_raw[:].rearrange("p (h w) n -> p w h n", w=3)
            nc.scalar.copy(wqk_hi[:, 0], v[:, 0])
            nc.scalar.copy(wqk_hi[:, 1], v[:, 1])
            nc.scalar.copy(wv_hi[:].rearrange("p (h n) -> p h n", h=H), v[:, 2]).then_inc(s_hi, 1)

        @block.vector
        def _(dve):
            nc.vector.memset(bias_rows[:], 0.0).then_inc(zeroed, 1)
            nc.vector.memset(tok_blocks[:], 0.0).then_inc(zeroed, 1)
            nc.vector.memset(ones[:], 1.0).then_inc(zeroed, 1)
            nc.vector.memset(one_b[:], 1.0).then_inc(zeroed, 1)
            done = [0]
            chain = s_chain

            def then(ins):
                done[0] += 1
                ins.then_inc(chain, 1)
                dve.wait_ge(chain, done[0])

            dve.wait_ge(loaded, 16)
            dve.wait_ge(zeroed, N_ZEROED)
            then(nc.vector.tensor_copy(tok[:], tok_i[:]))
            for mark, codes in ((opens, (40.0, 123.0, 91.0)), (closes, (41.0, 125.0, 93.0))):
                then(nc.vector.tensor_scalar(mark[:], tok[:], codes[0], None, ALU.is_equal))
                for code in codes[1:]:
                    then(nc.vector.scalar_tensor_tensor(out=mark[:], in0=tok[:], scalar=code, in1=mark[:],
                                                        op0=ALU.is_equal, op1=ALU.add))
            then(nc.vector.tensor_tensor(opens[:], opens[:], closes[:], ALU.subtract))
            then(nc.vector.tensor_tensor_scan(runs[:], one_b[:], opens[:], 0.0, ALU.mult, ALU.add))
            then(nc.vector.tensor_tensor_scan(low[:], runs[:], runs[:], 0.0, ALU.min, ALU.min))
            then(nc.vector.tensor_tensor(opens[:], runs[:], low[:], ALU.subtract))
            then(nc.vector.tensor_scalar(idx[:, 0, :], opens[:], 0.0, float(NEST - 1), ALU.max, ALU.min))
            then(nc.vector.tensor_scalar(closes[:], tok[:], 39990.0, None, ALU.is_gt))
            then(nc.vector.tensor_tensor_scan(runs[:], one_b[:], closes[:], 0.0, ALU.mult, ALU.add))
            then(nc.vector.tensor_copy(low[:], runs[:]))
            for m in range(8, TXT + 1, 8):
                then(nc.vector.tensor_scalar(closes[:], runs[:], float(m), -8.0, ALU.is_ge, ALU.mult))
                then(nc.vector.tensor_tensor(low[:], low[:], closes[:], ALU.add))
            nc.vector.tensor_copy(idx[:, 1, :], low[:]).then_inc(s_dve, 1)
            dve.wait_ge(s_turned, 1)
            nc.vector.tensor_copy(gate_w[:], work[:, 0, 0:2 + E])
            nc.vector.tensor_copy(pos_t[:], work[:, 0, 16:16 + TXT])
            nc.vector.memset(tabs_n[:, NEST:], 0.0)
            nc.vector.memset(tabs_s[:, 0:NEST], 0.0)
            nc.vector.tensor_copy(tabs_n[:, 0:NEST], work[:, 0, 128:128 + NEST])
            nc.vector.tensor_copy(tabs_s[:, NEST:], work[:, 0, 128 + NEST:128 + NEST + SEG]).then_inc(s_taken, 1)
            dve.wait_ge(s_turned, 2)
            then(nc.vector.tensor_copy(idx_t[:].rearrange("p a b -> p (a b)"), work[0:TXT, 1, 0:2 * B]))
            dve.wait_ge(s_pool, 3)
            for w, (a, n) in enumerate(((0, NEST), (NEST, SEG))):
                last = nc.vector.tensor_tensor(onehot[:, :, a:a + n],
                                               idx_t[:, w, :].unsqueeze(2).broadcast_to((TXT, B, n)),
                                               iota_e[:, 0:n].unsqueeze(1).broadcast_to((TXT, B, n)), ALU.is_equal)
            last.then_inc(s_taken, 1)
            dve.wait_ge(s_turned, 3)
            then(nc.vector.tensor_copy(base[:], work[0:TXT, 2, 0:D]))
            nc.vector.tensor_copy(rows24[:], work[0:NEST + SEG, 2, D:2 * D]).then_inc(s_taken, 1)
            for g in range(4):
                dve.wait_ge(s_turned, 4 + g)
                nc.vector.tensor_copy(hot_t[:, 4 * g:4 * g + 4, :].rearrange("p a b -> p (a b)"),
                                      scores[0:NEST + SEG, g // 2, g % 2, 0:4 * TXT]).then_inc(s_taken, 1)
            for g in range(4):
                dve.wait_ge(s_turned, 8 + g)
                ins = nc.vector.tensor_tensor(text_h[:, 4 * g:4 * g + 4, :],
                                              scores[0:TXT, g // 2, g % 2, :].rearrange("p (a b) -> p a b", a=4),
                                              base[:].unsqueeze(1).broadcast_to((TXT, 4, D)), ALU.add)
                if g == 3:
                    ins.then_inc(s_text, 1)
            for g, group in enumerate(groups):
                dve.wait_ge(s_turned, 12 + g)
                n = len(group) * P
                then(nc.vector.tensor_copy(turned[:, g % 4, 0:n], work[:, g % LANES, 0:n]))
                if g < 2:
                    then(nc.vector.tensor_copy(up_hi[:, g].rearrange("p a n -> p (a n)"), turned[:, g % 4, :]))
                    nc.vector.tensor_tensor(up_lo[:, g].rearrange("p a n -> p (a n)"), turned[:, g % 4, :],
                                            up_hi[:, g].rearrange("p a n -> p (a n)"), ALU.subtract).then_inc(s_taken, 1)
                    continue
                for i in range(len(group)):
                    m = 4 * (g - 2) + i
                    e, k = m // KC, m % KC
                    src = turned[:, g % 4, i * P:(i + 1) * P]
                    if e == 0:
                        ins = nc.vector.tensor_copy(down_sh[:, k, :], src)
                    else:
                        hi, lo = down_hi[:, k, (e - 1) * D:e * D], down_lo[:, k, (e - 1) * D:e * D]
                        then(nc.vector.tensor_copy(hi, src))
                        ins = nc.vector.tensor_tensor(lo, src, hi, ALU.subtract)
                    if i < len(group) - 1:
                        then(ins)
                ins.then_inc(s_taken, 1)
            dve.wait_ge(s_hi, 1)
            v = attn_raw[:].rearrange("p (h w) n -> p w h n", w=3)
            nc.vector.tensor_tensor(wqk_lo[:, 0], v[:, 0], wqk_hi[:, 0], ALU.subtract)
            nc.vector.tensor_tensor(wqk_lo[:, 1], v[:, 1], wqk_hi[:, 1], ALU.subtract)
            nc.vector.tensor_tensor(wv_lo[:].rearrange("p (h n) -> p h n", h=H), v[:, 2],
                                    wv_hi[:].rearrange("p (h n) -> p h n", h=H), ALU.subtract)

    yt_hi = sb(ctx, "yt_hi", [P, TW], F32R)
    yt_lo = sb(ctx, "yt_lo", [P, TW], F32R)
    q_a = [[sb(ctx, f"q_a{r}{i}", [P, TP], F32R) for i in range(2)] for r in range(2)]
    k_a = [[sb(ctx, f"k_a{r}{i}", [P, TP], F32R) for i in range(2)] for r in range(2)]
    q_b = [[sb(ctx, f"q_b{r}{i}", [P, TP], F32R) for i in range(2)] for r in range(2)]
    k_b = [[sb(ctx, f"k_b{r}{i}", [P, TP], F32R) for i in range(2)] for r in range(2)]
    values = sb(ctx, "values", [P, NT, H * DH])
    probs = sb(ctx, "probs", [P, NP, 2, CHUNK])
    sums = sb(ctx, "sums", [P, 2, 2, CHUNK])
    heads_t = sb(ctx, "heads_t", [P, PAIRS, TW])
    part_max = sb(ctx, "part_max", [P, 2 * NT, NC])
    neg_max = sb(ctx, "neg_max", [P, 2 * NT])
    max_rows = sb(ctx, "max_rows", [2 * NT, P], F32R)
    h_in = sb(ctx, "h_in", [P, NT, D])
    h_out = sb(ctx, "h_out", [P, NT, D])
    normed = sb(ctx, "normed", [P, NT * D])
    x_t = normed[:, 0:2 * P]
    counts = sb(ctx, "counts", [P, 12, 32])
    counts_t = sb(ctx, "counts_t", [P, 3 * P])
    flat_hi = sb(ctx, "flat_hi", [P, 2, GW], F32R)
    flat_lo = sb(ctx, "flat_lo", [P, 2, GW], F32R)
    hid = sb(ctx, "hid", [P, 2, KC, GW])
    hid_hi = sb(ctx, "hid_hi", [P, KC, GW], F32R)
    hid_lo = sb(ctx, "hid_lo", [P, KC, GW], F32R)
    stats = sb(ctx, "stats", [P, NT, 6])
    mean2 = [sb(ctx, f"mean2_{n}", [P, NT]) for n in range(2)]
    mdiff = sb(ctx, "mdiff", [P, NT])
    msq = sb(ctx, "msq", [P, NT])
    var = [sb(ctx, f"var_{n}", [P, NT]) for n in range(2)]
    minus_half = sb(ctx, "minus_half", [P, NT])
    rstd = [sb(ctx, f"rstd_{n}", [P, NT]) for n in range(2)]
    shift = [sb(ctx, f"shift_{n}", [P, NT]) for n in range(2)]
    logits = sb(ctx, "logits", [P, NT, 2 + E])
    g_on = sb(ctx, "g_on", [P, 2, NT])
    e_sel = sb(ctx, "e_sel", [P, NT, EG])
    e_tmp = sb(ctx, "e_tmp", [P, NT, EG])
    e_exp = sb(ctx, "e_exp", [P, NT, EG])
    e_max = sb(ctx, "e_max", [P, NT])
    rank = sb(ctx, "rank", [P, NT, EG])
    beats = sb(ctx, "beats", [P, 3, NT, 3])
    four = sb(ctx, "four", [P, EG])
    den = sb(ctx, "den", [P, 2, NT])
    comb = sb(ctx, "comb", [P, NT, E])

    filled = [sem(f"work_filled{k}") for k in range(LANES)]
    drained = [sem(f"work_drained{k}") for k in range(LANES)]
    x_loaded = sem("x_loaded")
    seeded = sem("seeded")
    resid_stored = sem("resid_stored")
    resid_loaded = sem("resid_loaded")
    out_stored = sem("out_stored")
    max_loaded = sem("max_loaded")
    scores_ready = sem("scores_ready")
    probs_ready = sem("probs_ready")
    probs_used = sem("probs_used")
    sums_done = sem("sums_done")
    heads_out = sem("heads_out")
    qk_hi = sem("qk_hi")
    max_ready = sem("max_ready")
    yt_hi_ready = sem("yt_hi_ready")
    var_ready = [sem(f"var_ready{n}") for n in range(2)]
    rstd_ready = [sem(f"rstd_ready{n}") for n in range(2)]
    shift_ready = [sem(f"shift_ready{n}") for n in range(2)]
    norm_ready = [sem(f"norm_ready{n}") for n in range(2)]
    flat_split = sem("flat_split")
    sel_ready = sem("sel_ready")
    sel_exp = sem("sel_exp")
    counted = sem("counted")
    tanh_ready = sem("tanh_ready")
    hid_split = sem("hid_split")
    sp_passed = sem("sp_passed")
    prepared = sem("prepared")

    pro = Segment(False, False, True, [0] * LANES)
    first = Segment(True, False, True, pro.after(1))
    loop = Segment(True, True, True, first.after(1))
    last = Segment(True, True, False, loop.after(B - 2))
    epi = Segment(False, True, False, last.after(1))

    def wait(eng, s, v):
        if not isinstance(v, int) or v > 0:
            eng.wait_ge(s, v)

    def wait_filled(eng, seg, it, u):
        wait(eng, filled[seg.bank[u]], seg.value(it, u))

    def wait_drained(eng, seg, it, *units):
        for k in range(LANES):
            of_bank = [u for u in units if seg.bank[u] == k]
            if of_bank:
                wait(eng, drained[k], seg.value(it, max(of_bank, key=seg.order.get)))

    def wait_bank(eng, seg, it, u, *needed):
        wait(eng, drained[seg.bank[u]], seg.value(it, u) - 1)
        wait_drained(eng, seg, it, *[n for n in needed if seg.bank[n] != seg.bank[u]])

    def run(eng, step):
        def iteration(seg, it, b):
            for s in range(ALL):
                step(seg, it, b, s)
        iteration(pro, 0, -1)
        iteration(first, 0, 0)
        with eng.Fori(1, B - 1) as b:
            iteration(loop, b - 1, b)
        iteration(last, 0, B - 1)
        iteration(epi, 0, B)

    def cut(s):
        return s // STEPS, s % STEPS // NT, s % NT

    def summed(s):
        return (NT - 1) * (s // NT) + max(s % NT, 1)

    block = ctx.enter_context(nc.Block())

    @block.tensor
    def _(pe):
        def needs(u):
            if u[0] == "qk" and u[1:] == (0, "k", 0):
                return [("turn1", g) for g in range(3)]
            if u[0] == "max" and u[2:] == (0, 0, 0):
                return [("qk", u[1], what, c) for what in "kq" for c in range(NC)]
            if u == ("proj", 0):
                return [("sum", PAIRS * NC - 1)]
            if u[0] == "gate":
                return [("turn2", g) for g in range(3)]
            if u[0] == "shared":
                return [("up", u[1], 0, k, 1) for k in range(KC)] + [("count",)]
            if u[0] == "embed":
                return [("turnx",)]
            return []

        def unit(seg, it, b, u):
            k, kind = seg.bank[u], u[0]
            w = work[:, k, :]
            wait_bank(pe, seg, it, u, *needs(u))
            if kind == "v":
                j = u[1]
                for n, (y, wv) in enumerate(((yt_hi, wv_hi), (yt_lo, wv_hi), (yt_hi, wv_lo))):
                    mm = nc.tensor.matmul(w, y[:, j * P:(j + 1) * P], wv[:], start=(n == 0), stop=(n == 2))
            elif kind == "qk":
                _, p, what, c = u
                m = "qk".index(what)
                c0, cw = CHUNKS[c]
                for n, (wt, y) in enumerate(((wqk_hi, yt_hi), (wqk_hi, yt_lo), (wqk_lo, yt_hi))):
                    mm = nc.tensor.matmul(w[:, 0:cw], wt[:, m, 2 * p:2 * p + 2, :].rearrange("p a n -> p (a n)"),
                                          y[:, c0:c0 + cw], start=(n == 0), stop=(n == 2))
            elif kind == "max":
                _, p, i, j, c = u
                c0, cw = CHUNKS[c]
                n = queries(j)
                mm = nc.tensor.matmul(w[0:n, 0:cw], q_a[p % 2][i][:, j * P:j * P + n],
                                      k_a[p % 2][i][:, c0:c0 + cw], start=True, stop=True)
            elif kind == "maxrow":
                pe.wait_ge(max_ready, PAIRS * b + (u[1] - 1) % PAIRS + 2)
                mm = nc.tensor.transpose(w[0:2 * NT, 0:P], neg_max[:], ident[:])
            elif kind == "sum":
                q = u[1]
                bb = b - 1 if q == PAIRS * NC - 1 else b
                pe.wait_ge(sums_done, (NT - 1) * (PAIRS * NC * bb + q + 1))
                cw = CHUNKS[q % NC][1]
                for i in range(2):
                    mm = nc.tensor.matmul(w[64 * i:64 * i + 64, 0:cw], ones[:], sums[:, q % 2, i, 0:cw],
                                          start=True, stop=True)
            elif kind == "proj":
                g = u[1]
                for j in range(3 * g, 3 * g + 3):
                    for p in range(PAIRS):
                        mm = nc.tensor.matmul(w[:, (j - 3 * g) * D:(j - 3 * g + 1) * D],
                                              heads_t[:, p, j * P:(j + 1) * P], wo[:, p, :],
                                              start=(p == 0), stop=(p == PAIRS - 1))
            elif kind in ("turn1", "turn2"):
                g, n = u[1], int(kind == "turn2")
                item = b - 1 if n else b + 1
                pe.wait_ge(norm_ready[n], NT * item + 3 * g + 3)
                for j in range(3):
                    mm = nc.tensor.transpose(w[:, j * P:(j + 1) * P],
                                             normed[:, (3 * g + j) * P:(3 * g + j + 1) * P], ident[:])
            elif kind == "gate":
                for j in range(NT):
                    mm = nc.tensor.matmul(w[:, j * (2 + E):(j + 1) * (2 + E)], normed[:, j * P:(j + 1) * P],
                                          gate_w[:], start=True, stop=True)
            elif kind == "count":
                pe.wait_ge(counted, b)
                for g in range(3):
                    mm = nc.tensor.transpose(w[:, g * P:(g + 1) * P],
                                             counts[:, 4 * g:4 * g + 4, :].rearrange("p a n -> p (a n)"), ident[:])
            elif kind == "up":
                _, c, path, k2, half = u
                pe.wait_ge(flat_split, 3 * (b - 1) + c + 1)
                m = 2 * half + k2
                for n, (wt, y) in enumerate(((up_hi, flat_hi), (up_hi, flat_lo), (up_lo, flat_hi))):
                    mm = nc.tensor.matmul(w[:, 0:GW], wt[:, path, m, :], y[:, c % 2, :],
                                          start=(n == 0), stop=(n == 2))
            elif kind == "shared":
                c = u[1]
                for j in range(3):
                    t = 3 * c + j
                    o = w[:, j * D:(j + 1) * D]
                    for k2 in range(KC):
                        nc.tensor.matmul(o, hid[:, 0, k2, j * P:(j + 1) * P], down_sh[:, k2, :],
                                         start=(k2 == 0), stop=False)
                    mm = nc.tensor.matmul(o, counts_t[:, t // 4 * P:(t // 4 + 1) * P], bias_rows[:, t % 4, :],
                                          start=False, stop=True)
            elif kind == "expert":
                _, t, g = u
                pe.wait_ge(hid_split, 3 * KC * (b - 1) + KC * (t // 3 + 1))
                cols = slice(t % 3 * P, (t % 3 + 1) * P)
                ops = [(k2, h, wt) for k2 in range(KC)
                       for h, wt in ((hid_hi, down_hi), (hid_lo, down_hi), (hid_hi, down_lo))]
                for n, (k2, h, wt) in enumerate(ops):
                    mm = nc.tensor.matmul(w, h[:, k2, cols], wt[:, k2, g * EG * D:(g + 1) * EG * D],
                                          start=(n == 0), stop=(n == len(ops) - 1))
            elif kind == "turnx":
                pe.wait_ge(x_loaded, 16 * (b + 2))
                for g in range(2):
                    mm = nc.tensor.transpose(w[:, g * P:(g + 1) * P],
                                             counts[:, 4 * g:4 * g + 4, :].rearrange("p a n -> p (a n)"), ident[:])
            elif kind == "embed":
                g = u[1]
                mm = nc.tensor.matmul(w, x_t[:, g * P:(g + 1) * P], tok_blocks[:].rearrange("p a n -> p (a n)"),
                                      start=True, stop=True)
            mm.then_inc(filled[k], 1)

        def score(seg, b, s):
            p, c, t = cut(s)
            if s % STEPS == 0:
                pe.wait_ge(max_loaded, 64 * (PAIRS * b + p + 1))
            wait(pe, probs_ready, ALL * b + s - 1)
            c0, cw = CHUNKS[c]
            n = rows(t)
            for i in range(2):
                o = scores[0:n, s % 2, i, 0:cw]
                nc.tensor.matmul(o, k_a[p % 2][i][:, t * P:t * P + n], q_a[p % 2][i][:, c0:c0 + cw],
                                 start=True, stop=False)
                mm = nc.tensor.matmul(o, k_b[p % 2][i][:, t * P:t * P + n], q_b[p % 2][i][:, c0:c0 + cw],
                                      start=False, stop=True)
            mm.then_inc(scores_ready, 1)

        def weigh(seg, it, b, s):
            p, c, t = cut(s)
            pe.wait_ge(probs_ready, ALL * b + s + 1)
            if s < NT:
                wait_drained(pe, seg, it, ("v", t))
            if t == 0:
                wait(pe, heads_out, PAIRS * NC * b + s // NT)
            cw, n = CHUNKS[c][1], rows(t)
            for i in range(2):
                h = 2 * p + i
                mm = nc.tensor.matmul(o_ps[64 * i:64 * i + 64, 0:cw], values[0:n, t, h * DH:(h + 1) * DH],
                                      probs[0:n, s % NP, i, 0:cw], start=(t == 0), stop=(t == NT - 1))
            mm.then_inc(probs_used, 1)

        def step(seg, it, b, s):
            if seg.attn:
                score(seg, b, s)
                if s > 0:
                    weigh(seg, it, b, s - 1)
            for u in seg.at[s]:
                unit(seg, it, b, u)
            if seg.attn and s == ALL - 1:
                weigh(seg, it, b, s)

        pe.wait_ge(prepared, 1)
        run(pe, step)

    @block.scalar
    def _(act):
        def unit(seg, it, b, u):
            k, kind = seg.bank[u], u[0]
            w = work[:, k, :]
            if kind not in ("v", "qk", "turn1", "turn2", "count", "up", "turnx") or (kind == "up" and u[4]):
                return
            wait_filled(act, seg, it, u)
            if kind == "v":
                wait(act, probs_used, ALL * b)
                nc.scalar.copy(values[:, u[1], :], w).then_inc(drained[k], 1)
            elif kind == "qk":
                _, p, what, c = u
                c0, cw = CHUNKS[c]
                for i in range(2):
                    src = w[64 * i:64 * i + 64, 0:cw]
                    a, z = (k_a, k_a) if what == "k" else (q_a, q_b)
                    nc.scalar.copy(a[p % 2][i][0:64, c0:c0 + cw], src)
                    o = 64 if what == "k" else 0
                    ins = nc.scalar.copy(z[p % 2][i][o:o + 64, c0:c0 + cw], src)
                ins.then_inc(qk_hi, 1)
            elif kind == "turn1":
                g = u[1]
                nc.scalar.copy(yt_hi[:, g * GW:(g + 1) * GW], w[:, 0:GW]).then_inc(yt_hi_ready, 1)
            elif kind == "turn2":
                g = u[1]
                nc.scalar.activation(normed[:, g * GW:(g + 1) * GW], w[:, 0:GW], ACT.Identity,
                                     bias=ln_cols[:, 1:2], scale=ln_cols[:, 0:1]).then_inc(drained[k], 1)
            elif kind == "count":
                nc.scalar.copy(counts_t[:], w[:, 0:3 * P]).then_inc(drained[k], 1)
            elif kind == "turnx":
                nc.scalar.copy(x_t, w[:, 0:2 * P]).then_inc(drained[k], 1)
            elif kind == "up":
                _, c, path, k2, half = u
                nc.scalar.activation(hid[:, path, k2, :], w[:, 0:GW], ACT.Tanh, scale=0.5).then_inc(tanh_ready, 1)

        def normalise(n, item, src):
            act.wait_ge(shift_ready[n], item + 1)
            for j in range(NT):
                nc.scalar.activation(normed[:, j * D:(j + 1) * D], src[:, j, :], ACT.Identity,
                                     bias=shift[n][:, j:j + 1], scale=rstd[n][:, j:j + 1]).then_inc(norm_ready[n], 1)

        def heads(seg, it, b, q):
            act.wait_ge(probs_used, ALL * b + NT * (q + 1))
            if q == 0 and seg.post:
                wait_filled(act, seg, it, ("proj", 2))
            c0, cw = CHUNKS[q % NC]
            nc.scalar.copy(heads_t[:, q // NC, c0:c0 + cw], o_ps[:, 0:cw]).then_inc(heads_out, 1)

        def step(seg, it, b, s):
            if seg.attn:
                p, c, t = cut(s)
                act.wait_ge(scores_ready, ALL * b + s + 1)
                wait(act, probs_used, ALL * b + s - NP + 1)
                if not isinstance(b, int) or b > 0 or s >= NP:
                    wait(act, sums_done, (NT - 1) * PAIRS * NC * b + summed(s - NP))
                cw, n = CHUNKS[c][1], rows(t)
                nc.scalar.activation(probs[0:n, s % NP, :, 0:cw], scores[0:n, s % 2, :, 0:cw], ACT.Exp,
                                     scale=DH ** -0.5).then_inc(probs_ready, 1)
                if t == 0 and s > 0:
                    heads(seg, it, b, s // NT - 1)
            if seg.post and s == 11:
                normalise(1, b - 1, h_out)
            if seg.prep and s == 63:
                normalise(0, b + 1, h_in)
            if seg.post and s == 20:
                act.wait_ge(sel_ready, b)
                nc.scalar.activation(e_exp[:], e_sel[:], ACT.Exp).then_inc(sel_exp, 1)
            for u in seg.at[s]:
                unit(seg, it, b, u)
            if seg.attn and s == ALL - 1:
                heads(seg, it, b, PAIRS * NC - 1)

        act.wait_ge(prepared, 1)
        run(act, step)

    @block.vector
    def _(dve):
        done = [0]

        def then(ins):
            done[0] += 1
            ins.then_inc(s_chain, 1)
            dve.wait_ge(s_chain, done[0])

        def unit(seg, it, b, u):
            k, kind = seg.bank[u], u[0]
            w = work[:, k, :]
            if kind in ("v", "turn2", "count", "turnx"):
                return
            wait_filled(dve, seg, it, u)
            if kind == "qk":
                _, p, what, c = u
                c0, cw = CHUNKS[c]
                n = 6 * (PAIRS * b + (p - 1) % PAIRS + 1) + 3 * "kq".index(what) + c + 1
                dve.wait_ge(qk_hi, n)
                for i in range(2):
                    src = w[64 * i:64 * i + 64, 0:cw]
                    if what == "k":
                        ins = nc.vector.tensor_tensor(k_b[p % 2][i][0:64, c0:c0 + cw], src,
                                                      k_a[p % 2][i][0:64, c0:c0 + cw], ALU.subtract)
                    else:
                        ins = nc.vector.tensor_tensor(q_a[p % 2][i][64:128, c0:c0 + cw], src,
                                                      q_b[p % 2][i][0:64, c0:c0 + cw], ALU.subtract)
                ins.then_inc(drained[k], 1)
            elif kind == "max":
                _, p, i, j, c = u
                n = queries(j)
                keys = min(CHUNKS[c][1], T - CHUNKS[c][0])
                nc.vector.tensor_reduce(part_max[0:n, i * NT + j, c:c + 1], w[0:n, 0:keys], AX.X,
                                        ALU.max).then_inc(drained[k], 1)
                if (i, j, c) == (1, NT - 1, NC - 1):
                    wait_drained(dve, seg, it, u)
                    nc.vector.tensor_reduce(neg_max[:], part_max[:], AX.X, ALU.max, negate=True).then_inc(max_ready, 1)
            elif kind == "maxrow":
                wait(dve, max_loaded, 64 * (PAIRS * b + (u[1] - 1) % PAIRS + 1))
                nc.vector.tensor_copy(max_rows[:], w[0:2 * NT, 0:P]).then_inc(drained[k], 1)
            elif kind == "sum":
                q = u[1]
                n = PAIRS * NC * (b - 1 if q == PAIRS * NC - 1 else b) + q
                c0, cw = CHUNKS[q % NC]
                then(nc.vector.reciprocal(w[:, 0:cw], w[:, 0:cw]))
                dve.wait_ge(heads_out, n + 1)
                o = heads_t[:, q // NC, c0:c0 + cw]
                nc.vector.tensor_tensor(o, w[:, 0:cw], o, ALU.mult).then_inc(drained[k], 1)
            elif kind == "proj":
                g = u[1]
                dve.wait_ge(resid_loaded, 16 * b)
                o = h_out[:, 3 * g:3 * g + 3, :].rearrange("p a n -> p (a n)")
                nc.vector.tensor_tensor(o, w[:, 0:GW], o, ALU.add).then_inc(drained[k], 1)
            elif kind == "turn1":
                g = u[1]
                dve.wait_ge(yt_hi_ready, 3 * (b + 1) + g + 1)
                cols = slice(g * GW, (g + 1) * GW)
                nc.vector.tensor_tensor(yt_lo[:, cols], w[:, 0:GW], yt_hi[:, cols], ALU.subtract).then_inc(drained[k], 1)
            elif kind == "gate":
                nc.vector.tensor_tensor(logits[:], w[:, 0:NT * (2 + E)].rearrange("p (a n) -> p a n", a=NT),
                                        gate_b[:].unsqueeze(1).broadcast_to((P, NT, 2 + E)),
                                        ALU.add).then_inc(drained[k], 1)
                wait_drained(dve, seg, it, u)
                choose()
            elif kind == "up":
                _, c, path, k2, half = u
                o = hid[:, path, k2, :]
                if half == 0:
                    dve.wait_ge(tanh_ready, 12 * (b - 1) + 4 * c + 2 * path + k2 + 1)
                    nc.vector.scalar_tensor_tensor(out=o, in0=o, scalar=1.0, in1=w[:, 0:GW], op0=ALU.add,
                                                   op1=ALU.mult).then_inc(drained[k], 1)
                else:
                    wait_drained(dve, seg, it, ("up", c, path, k2, 0))
                    nc.vector.scalar_tensor_tensor(out=o, in0=o, scalar=0.5, in1=w[:, 0:GW], op0=ALU.mult,
                                                   op1=ALU.mult).then_inc(drained[k], 1)
                    if path == 1:
                        wait_drained(dve, seg, it, u)
                        then(nc.vector.tensor_copy(hid_hi[:, k2, :], o))
                        nc.vector.tensor_tensor(hid_lo[:, k2, :], o, hid_hi[:, k2, :],
                                                ALU.subtract).then_inc(hid_split, 1)
                if u == ("up", 0, 1, 1, 1):
                    split_flat(seg, it, 2)
            elif kind == "shared":
                c = u[1]
                o = h_out[:, 3 * c:3 * c + 3, :].rearrange("p a n -> p (a n)")
                nc.vector.tensor_tensor(o, w[:, 0:GW], o, ALU.add).then_inc(drained[k], 1)
            elif kind == "expert":
                _, t, g = u
                wait_drained(dve, seg, it, ("expert", t, 0) if g else ("shared", t // 3))
                o = h_out[:, t, :]
                for e in range(EG):
                    ins = nc.vector.scalar_tensor_tensor(
                        out=o, in0=w[:, e * D:(e + 1) * D], scalar=comb[:, t, g * EG + e:g * EG + e + 1],
                        in1=o, op0=ALU.mult, op1=ALU.add)
                    if e < EG - 1:
                        then(ins)
                ins.then_inc(drained[k], 1)
            elif kind == "embed":
                g = u[1]
                wait(dve, seeded, 32 * (b + 2))
                o = h_in[:, 4 * g:4 * g + 4, :].rearrange("p a n -> p (a n)")
                nc.vector.tensor_tensor(o, w, o, ALU.add).then_inc(drained[k], 1)

        def split_flat(seg, it, c):
            wait_drained(dve, seg, it, ("turn2", c))
            src = normed[:, c * GW:(c + 1) * GW]
            then(nc.vector.tensor_copy(flat_hi[:, c % 2, :], src))
            nc.vector.tensor_tensor(flat_lo[:, c % 2, :], src, flat_hi[:, c % 2, :], ALU.subtract).then_inc(flat_split, 1)

        def statistics(n, src):
            for j in range(NT):
                ins = nc.vector.bn_stats(stats[:, j, :], src[:, j, :])
            then(ins)
            nc.vector.tensor_tensor(mean2[n][:], stats[:, :, 1], stats[:, :, 4], ALU.add)
            nc.vector.tensor_tensor(msq[:], stats[:, :, 2], stats[:, :, 5], ALU.add)
            then(nc.vector.tensor_tensor(mdiff[:], stats[:, :, 1], stats[:, :, 4], ALU.subtract))
            then(nc.vector.scalar_tensor_tensor(out=mdiff[:], in0=mdiff[:], scalar=0.25, in1=mdiff[:],
                                                op0=ALU.mult, op1=ALU.mult))
            ins = nc.vector.scalar_tensor_tensor(out=var[n][:], in0=msq[:], scalar=1.0 / D, in1=mdiff[:],
                                                 op0=ALU.mult, op1=ALU.add)
            then(ins)
            scale, eps = (1.0 + EPS, EPS * EPS) if n else (1.0, EPS)
            nc.vector.tensor_scalar(var[n][:], var[n][:], scale, eps, ALU.mult, ALU.add).then_inc(var_ready[n], 1)

        def shifts(n, item):
            dve.wait_ge(rstd_ready[n], item + 1)
            nc.vector.scalar_tensor_tensor(out=shift[n][:], in0=mean2[n][:], scalar=-0.5, in1=rstd[n][:],
                                           op0=ALU.mult, op1=ALU.mult).then_inc(shift_ready[n], 1)

        def choose():
            nc.vector.tensor_tensor(g_on[:, 0, :], logits[:, :, 0], logits[:, :, 1], ALU.is_ge)
            then(nc.vector.tensor_tensor(g_on[:, 1, :], logits[:, :, 1], logits[:, :, 0], ALU.is_gt))
            for g, o in ((0, e_tmp), (1, e_sel)):
                ins = nc.vector.tensor_tensor(o[:], logits[:, :, 2 + g * EG:2 + (g + 1) * EG],
                                              g_on[:, g, :].unsqueeze(2).broadcast_to((P, NT, EG)), ALU.mult)
            then(ins)
            then(nc.vector.tensor_tensor(e_sel[:], e_sel[:], e_tmp[:], ALU.add))
            then(nc.vector.tensor_reduce(e_max[:], e_sel[:], AX.X, ALU.max))
            for d in (1, 2, 3):
                nc.vector.tensor_tensor(beats[:, d - 1, :, 0:EG - d], e_sel[:, :, d:], e_sel[:, :, 0:EG - d], ALU.is_gt)
            then(nc.vector.tensor_copy(rank[:], four[:].unsqueeze(1).broadcast_to((P, NT, EG))))
            nc.vector.tensor_tensor(e_sel[:], e_sel[:], e_max[:].unsqueeze(2).broadcast_to((P, NT, EG)),
                                    ALU.subtract).then_inc(sel_ready, 1)
            for d in (1, 2, 3):
                m = beats[:, d - 1, :, 0:EG - d]
                then(nc.vector.tensor_tensor(rank[:, :, 0:EG - d], rank[:, :, 0:EG - d], m, ALU.add))
                then(nc.vector.tensor_tensor(rank[:, :, d:], rank[:, :, d:], m, ALU.subtract))
            then(nc.vector.tensor_scalar(rank[:], rank[:], 1.5, None, ALU.is_lt))

        def weights(b):
            for g in range(2):
                nc.vector.tensor_tensor(counts[:, 0:NT, g * EG:(g + 1) * EG], rank[:],
                                        g_on[:, g, :].unsqueeze(2).broadcast_to((P, NT, EG)), ALU.mult)
            nc.vector.memset(counts[:, 0:NT, E:E + 1], 1.0).then_inc(counted, 1)
            dve.wait_ge(sel_exp, b)
            nc.vector.tensor_tensor(e_tmp[:], e_exp[:], rank[:], ALU.mult)
            then(nc.vector.tensor_reduce(den[:, 0, :], e_exp[:], AX.X, ALU.add))
            then(nc.vector.tensor_reduce(den[:, 1, :], e_tmp[:], AX.X, ALU.add))
            then(nc.vector.scalar_tensor_tensor(out=den[:, 0, :], in0=den[:, 0, :], scalar=1e-8, in1=den[:, 1, :],
                                                op0=ALU.mult, op1=ALU.add))
            then(nc.vector.reciprocal(den[:, 1, :], den[:, 0, :]))
            then(nc.vector.tensor_tensor(e_tmp[:], e_tmp[:], den[:, 1, :].unsqueeze(2).broadcast_to((P, NT, EG)),
                                         ALU.mult))
            for g in range(2):
                ins = nc.vector.tensor_tensor(comb[:, :, g * EG:(g + 1) * EG], e_tmp[:],
                                              g_on[:, g, :].unsqueeze(2).broadcast_to((P, NT, EG)), ALU.mult)
            then(ins)

        def step(seg, it, b, s):
            if s == 0:
                if done[0]:
                    nc.vector.sem_clear(s_chain)
                done[0] = 0
            for u in seg.at[s]:
                unit(seg, it, b, u)
            if seg.post:
                if s == 8:
                    wait_drained(dve, seg, it, *[("proj", g) for g in range(3)])
                    statistics(1, h_out)
                if s == 10:
                    shifts(1, b - 1)
                if s in (16, 17):
                    split_flat(seg, it, s - 16)
                if s == 21:
                    weights(b)
            if seg.prep:
                if s == 59:
                    wait_drained(dve, seg, it, ("embed", 1))
                    statistics(0, h_in)
                if s == 62:
                    shifts(0, b + 1)

        nc.vector.sem_clear(s_chain)
        for r in range(2):
            for i in range(2):
                nc.vector.memset(q_b[r][i][64:128, :].bitcast(F32), 0.0)
                then(nc.vector.memset(k_b[r][i][64:128, :].bitcast(F32), 0.0))
                nc.vector.memset(k_b[r][i][64:65, :].bitcast(F32), 1.0)
        nc.vector.memset(heads_t[:], 0.0)
        nc.vector.memset(part_max[:], 0.0)
        nc.vector.memset(h_in[:], 0.0)
        nc.vector.memset(minus_half[:], -0.5)
        nc.vector.memset(four[:, 0:1], 0.0)
        nc.vector.memset(four[:, 1:2], 1.0)
        nc.vector.memset(four[:, 2:3], 2.0)
        nc.vector.memset(four[:, 3:4], 3.0)
        nc.vector.memset(counts[:], 0.0).then_inc(prepared, 1)
        dve.wait_ge(prepared, 1)
        run(dve, step)

    @block.gpsimd
    def _(pool):
        def root(n, item):
            pool.wait_ge(var_ready[n], item + 1)
            nc.gpsimd.tensor_tensor(rstd[n][:], var[n][:], minus_half[:], ALU.pow).then_inc(rstd_ready[n], 1)

        def step(seg, it, b, s):
            if seg.post and s == 9:
                root(1, b - 1)
            if seg.prep and s == 60:
                root(0, b + 1)
            if not seg.attn:
                return
            p, c, t = cut(s)
            if t == 0:
                return
            q = s // NT
            cw, n = CHUNKS[c][1], rows(t)
            pool.wait_ge(probs_ready, ALL * b + s + 1)
            acc = sums[0:n, q % 2, :, 0:cw]
            if t == 1:
                nc.gpsimd.tensor_tensor(acc, probs[:, (s - 1) % NP, :, 0:cw], probs[:, s % NP, :, 0:cw],
                                        ALU.add).then_inc(sums_done, 1)
            else:
                pool.wait_ge(sums_done, (NT - 1) * (PAIRS * NC * b + q) + t - 1)
                nc.gpsimd.tensor_tensor(acc, acc, probs[0:n, s % NP, :, 0:cw], ALU.add).then_inc(sums_done, 1)

        pool.wait_ge(prepared, 1)
        run(pool, step)

    @block.sync
    def _(sp):
        def wait_then(sem_wait, *args):
            sem_wait(*args)
            sp.sem_inc(sp_passed, 1)

        x_rows = x.rearrange("b h w f -> b (h w) f").rearrange("b (p j) f -> b p j f", j=IMG)
        out_img = out[:, 0:HW, :].rearrange("b (p j) d -> b p j d", j=IMG)

        def seed(n):
            sp.dma_start(h_in[:, 0:IMG, :], pe_table.rearrange("(p j) d -> p j d", j=IMG)).then_inc(seeded, 16)
            sp.dma_start(h_in[0:TXT, IMG, :], text_dram[n]).then_inc(seeded, 16)

        def step(seg, it, b, s):
            if seg.post and s == 0:
                wait_then(sp.wait_ge, resid_stored, 16 * b)
                sp.dma_start(h_out[:].rearrange("p a n -> p (a n)"), resid_dram[b - 1]).then_inc(resid_loaded, 16)
            if seg.prep and s == 30:
                if seg.post:
                    wait_then(wait_drained, sp, seg, it, ("count",))
                sp.dma_start(counts[:, 0:IMG, 0:F], x_rows[b + 1]).then_inc(x_loaded, 16)
                wait_then(wait, sp, norm_ready[0], NT * (b + 1))
                seed(b + 1)
            if seg.prep and s == 62:
                wait_then(wait_drained, sp, seg, it, ("embed", 1))
                sp.dma_start(resid_dram[b + 1], h_in[:].rearrange("p a n -> p (a n)")).then_inc(resid_stored, 16)
                wait_then(sp.wait_ge, resid_stored, 16 * (b + 2))
            for u in seg.at[s]:
                if u[0] == "maxrow":
                    wait_then(wait_drained, sp, seg, it, u)
                    for i in range(2):
                        row = q_b[u[1] % 2][i][64:65, :].bitcast(F32)
                        r = i * NT
                        sp.dma_start(row[:, 0:HW].rearrange("p (a n) -> p a n", a=IMG),
                                     max_rows[r:r + IMG, :].bitcast(F32)).then_inc(max_loaded, 16)
                        sp.dma_start(row[:, HW:TP], max_rows[r + IMG:r + NT, 0:TP - HW].bitcast(F32)).then_inc(max_loaded, 16)
            if seg.post and s == 80:
                wait_then(wait_drained, sp, seg, it, ("expert", NT - 1, 1))
                sp.dma_start(out_img[b - 1], h_out[:, 0:IMG, :]).then_inc(out_stored, 16)
                sp.dma_start(out[b - 1, HW:T, :], h_out[0:TXT, IMG, :]).then_inc(out_stored, 16)
                wait_then(sp.wait_ge, out_stored, 32 * b)

        sp.wait_ge(prepared, 1)
        run(sp, step)

    ctx.close()


_INS = ['x', 'x_txt', 'L0_tok_W', 'L0_txt_pos_table', 'L0_txt_nest_table', 'L0_txt_seg_table', 'L0_txt_W',
        'L0_attn_kernel', 'L0_attn_head_kernel', 'L0_ffn_ln_scale', 'L0_ffn_ln_bias', 'L0_ffn_shared_in_w',
        'L0_ffn_shared_out_w', 'L0_ffn_shared_out_b', 'L0_ffn_expert_in_w', 'L0_ffn_expert_out_weight',
        'L0_ffn_expert_out_bias', 'L0_ffn_group_gate_w', 'L0_ffn_expert_gate_w', 'L0_ffn_group_bias',
        'L0_ffn_expert_bias']


def position_table():
    position = np.arange(HW, dtype=np.float32)[:, None]
    div_term = np.exp(np.arange(0, D, 2, dtype=np.float32) * np.float32(-np.log(10000.0) / D))
    table = np.zeros((HW, D), dtype=np.float32)
    table[:, 0::2] = np.sin(position * div_term)
    table[:, 1::2] = np.cos(position * div_term)
    return table


def kernel(**inputs):
    import concourse.bacc as bacc
    from concourse.bass_utils import run_bass_kernel_spmd

    nc = bacc.Bacc("TRN2", target_bir_lowering=False, num_devices=1)
    arrays, args = {}, []
    for name in _INS + ["pe_table"]:
        a = np.ascontiguousarray(inputs[name] if name in inputs else position_table())
        arrays[f"in_{name}_dram"] = a
        args.append(nc.dram_tensor(f"in_{name}_dram", a.shape, mybir.dt.from_np(a.dtype), kind="ExternalInput").ap())
    args.append(nc.dram_tensor("out_0_dram", (B, T, D), F32, kind="ExternalOutput").ap())
    fusion_kernel(nc, *args)
    r = run_bass_kernel_spmd(nc, [arrays], core_ids=[0])
    return r.results[0]["out_0_dram"]
```

```python
from contextlib import ExitStack

import numpy as np

import concourse.bass as bass
from concourse import mybir
from concourse.alu_op_type import AluOpType as ALU

F32 = mybir.dt.float32
F32R = mybir.dt.float32r
I32 = mybir.dt.int32
ACT = mybir.ActivationFunctionType
AX = mybir.AxisListType

P = 128
B, HW, F = 16, 1024, 29
TXT = 77
T = HW + TXT
TP = T + 1
IMG = HW // P
NT = IMG + 1
TW = NT * P
D = 128
H, DH = 8, 64
PAIRS = H // 2
CHUNK = 368
CHUNKS = [(0, CHUNK), (CHUNK, CHUNK), (2 * CHUNK, TP - 2 * CHUNK)]
NC = len(CHUNKS)
STEPS = NC * NT
ALL = PAIRS * STEPS
GW = 3 * P
E, EG, HID = 8, 4, 256
KC = HID // P
EPS = 1e-5
NEST, SEG = 16, 8
LANES = 3
NP = 2
PROJ = [4 + j for j in range(NT)]
STATS, TURN, GATE, WEIGHTS = 13, 16, 20, 23
EMBED = 58
MAXROW = 22
STORE = 102
PAUSE = ("pause",)


def rows(t):
    return P if t < IMG else TXT


def queries(j):
    return P if j < IMG else TP - IMG * P


LOAD = {"v": (65, 0, 50), "qk": (48, 95, 130), "max": (16, 50, 0), "maxrow": (10, 50, 0), "sum": (65, 0, 36),
        "proj": (88, 20, 0), "turn1": (30, 50, 50), "turn2": (30, 0, 50), "gate": (60, 180, 0),
        "count": (30, 0, 50), "up": (48, 60, 20), "upx": (48, 160, 0), "shared": (66, 20, 0),
        "expert": (135, 130, 0), "turnx": (20, 0, 40), "embed": (90, 70, 0)}
STEP = (130, 0, 70)


def projections(p):
    return [("qk", p, "kq"[n % 2], n // 2) for n in range(2 * NC)]


def maxima(p):
    units, first_need, seen = [], {}, set()
    for n in range(1, 2 * NC):
        c0, cw = CHUNKS[(n - 1) // 2]
        new = [("max", p, i, j, c) for i in range(2) for j in range(NT) for c in range(n // 2 + 1)
               if j * P + queries(j) <= c0 + cw and (i, j, c) not in seen]
        seen |= {u[2:] for u in new}
        first_need[new[0]] = projections(p)[0 if n == 1 else n:n + 1]
        units += new
    return units, first_need


def load(u):
    return LOAD["upx" if u[0] == "up" and u[2:] == (1, u[3], 1) else u[0]]


def plan(attn, post, prep):
    at = [[] for _ in range(ALL)]
    used = [list(STEP) if attn else [0, 0, 0] for _ in range(ALL)]

    def put(s, u):
        at[s].append(u)
        used[s] = [a + b for a, b in zip(used[s], load(u))]
        if u[0] == "sum":
            used[s + 1][1] += 125
            used[s + 2][1] += 170

    def fill(units, first, last, engine):
        def place(level):
            s, backlog, places = first, 0, []
            for u in units:
                while s <= last and (u == PAUSE or used[s][engine] + backlog >= level):
                    backlog = max(0, backlog + used[s][engine] - level)
                    s += 1
                    if u == PAUSE:
                        break
                if s > last:
                    return None
                if u != PAUSE:
                    places.append((s, u))
                    backlog += load(u)[engine]
            return places
        level = 50
        while place(level) is None:
            level += 2
        for s, u in place(level):
            put(s, u)

    if attn:
        for j in range(NT):
            put(j, ("v", j))
        for q in range(PAIRS * NC - 1):
            put(NT * (q + 1) + 2, ("sum", q))
    if post:
        put(1, ("sum", PAIRS * NC - 1))
        for j in range(NT):
            put(PROJ[j], ("proj", j))
        for g in range(3):
            used[PROJ[3 * g + 2] + 1][1] += 70
            put(TURN + g, ("turn2", g))
        used[STATS][1] += 70
        put(GATE, ("gate",))
        used[GATE + 1][1] += 200
        used[WEIGHTS][1] += 200
        put(WEIGHTS + 2, ("count",))
    if prep:
        put(EMBED, ("turnx",))
        for g in range(2):
            put(EMBED + 1 + g, ("embed", g))
        used[EMBED + 3][1] += 300
        for g in range(3):
            put(EMBED + 8 + g, ("turn1", g))
    for p in range(PAIRS):
        if (attn and p < PAIRS - 1) or (prep and p == PAIRS - 1):
            nxt = (p + 1) % PAIRS
            for n, u in enumerate(projections(nxt)):
                put(STEPS * p + n, u)
            fill(maxima(nxt)[0], STEPS * p + 3, STEPS * p + MAXROW - 1, 1)
            put(STEPS * p + MAXROW, ("maxrow", nxt))
    if post:
        units = []
        for c in range(3):
            units += [("up", c, path, k, half) for path in (1, 0) for k in range(KC) for half in range(2)]
            units += [PAUSE]
            for t in range(3 * c, 3 * c + 3):
                units += [("shared", t), ("expert", t, 0), ("expert", t, 1)]
        fill(units, WEIGHTS + 3, STORE - 2, 0)
    return at


class Segment:

    def __init__(self, attn, post, prep, before):
        self.attn, self.post, self.prep = attn, post, prep
        self.at = plan(attn, post, prep)
        self.before = before
        self.uses = [0] * LANES
        self.bank, self.order = {}, {}
        n = 0
        for units in self.at:
            for u in units:
                k = n % LANES
                self.bank[u] = k
                self.uses[k] += 1
                self.order[u] = self.uses[k]
                n += 1

    def after(self, times):
        return [b + times * u for b, u in zip(self.before, self.uses)]

    def value(self, it, u):
        k = self.bank[u]
        return it * self.uses[k] + self.before[k] + self.order[u]


def fusion_kernel(nc, x, x_txt, tok_w, pos, nest, seg, txt_w, attn_w, head_w, ln_scale, ln_bias,
                  sh_in, sh_out, sh_out_b, ex_in, ex_out, ex_out_b, group_w, expert_w,
                  group_b, expert_b, pe_table, out):
    ctx = ExitStack()
    text_dram = nc.dram_tensor("text_rows", (B, TXT, D), F32, kind="Internal").ap()
    resid_dram = nc.dram_tensor("resid_rows", (B, P, NT * D), F32, kind="Internal").ap()

    def sb(stack, name, shape, dt=F32):
        return stack.enter_context(nc.sbuf_tensor(name, shape, dt))

    def sem(name):
        return ctx.enter_context(nc.semaphore(name))

    scores = ctx.enter_context(nc.psum_tensor("scores", [P, 2, 2, 512], F32))
    o_ps = ctx.enter_context(nc.psum_tensor("o_ps", [P, 512], F32))
    work = ctx.enter_context(nc.psum_tensor("work", [P, LANES, 512], F32))

    ident = sb(ctx, "ident", [P, P])
    ones = sb(ctx, "ones", [P, DH])
    wqk_hi = sb(ctx, "wqk_hi", [P, 2, H, DH], F32R)
    wqk_lo = sb(ctx, "wqk_lo", [P, 2, H, DH], F32R)
    wv_hi = sb(ctx, "wv_hi", [P, H * DH], F32R)
    wv_lo = sb(ctx, "wv_lo", [P, H * DH], F32R)
    wo = sb(ctx, "wo", [P, PAIRS, D])
    up_hi = sb(ctx, "up_hi", [P, 2, 4, P], F32R)
    up_lo = sb(ctx, "up_lo", [P, 2, 4, P], F32R)
    down_hi = sb(ctx, "down_hi", [P, KC, E * D], F32R)
    down_lo = sb(ctx, "down_lo", [P, KC, E * D], F32R)
    down_sh = sb(ctx, "down_sh", [P, KC, D])
    gate_w = sb(ctx, "gate_w", [P, 2 + E])
    gate_b = sb(ctx, "gate_b", [P, 2 + E])
    ln_cols = sb(ctx, "ln_cols", [P, 2])
    bias_rows = sb(ctx, "bias_rows", [P, 4, D])
    tok_blocks = sb(ctx, "tok_blocks", [P, 4, D])

    loaded = sem("loaded")
    zeroed = sem("zeroed")
    raw_loaded = sem("raw_loaded")
    s_pool = sem("s_pool")
    s_turned = sem("s_turned")
    s_taken = sem("s_taken")
    s_dve = sem("s_dve")
    s_text = sem("s_text")
    s_hi = sem("s_hi")
    s_stored = sem("s_stored")
    s_chain = sem("s_chain")

    with ExitStack() as tmp:
        attn_raw = sb(tmp, "attn_raw", [P, 3 * H, DH])
        in_raw = sb(tmp, "in_raw", [P, 2, 4, D])
        out_raw = sb(tmp, "out_raw", [P, 1 + E, HID])
        gates_raw = sb(tmp, "gates_raw", [2 + E, D])
        pos_raw = sb(tmp, "pos_raw", [TXT, D])
        tab_raw = sb(tmp, "tab_raw", [NEST + SEG, D])
        txt_wr = sb(tmp, "txt_wr", [P, 3, D])
        turned = sb(tmp, "turned", [P, 4, 512])
        tabs_n = sb(tmp, "tabs_n", [P, NEST + SEG])
        tabs_s = sb(tmp, "tabs_s", [P, NEST + SEG])
        pos_t = sb(tmp, "pos_t", [P, TXT])
        base = sb(tmp, "base", [TXT, D])
        rows24 = sb(tmp, "rows24", [NEST + SEG, D])
        tok_i = sb(tmp, "tok_i", [B, TXT], I32)
        tok = sb(tmp, "tok", [B, TXT])
        opens = sb(tmp, "opens", [B, TXT])
        closes = sb(tmp, "closes", [B, TXT])
        one_b = sb(tmp, "one_b", [B, TXT])
        runs = sb(tmp, "runs", [B, TXT])
        low = sb(tmp, "low", [B, TXT])
        idx = sb(tmp, "idx", [B, 2, TXT])
        idx_t = sb(tmp, "idx_t", [TXT, 2, B])
        iota_e = sb(tmp, "iota_e", [TXT, NEST])
        onehot = sb(tmp, "onehot", [TXT, B, NEST + SEG])
        hot_t = sb(tmp, "hot_t", [NEST + SEG, B, TXT])
        text_h = sb(tmp, "text_h", [TXT, B, D])
        block = tmp.enter_context(nc.Block())

        N_ZEROED = 4

        @block.gpsimd
        def _(pool):
            nc.gpsimd.memset(ident[:], 0.0).then_inc(s_pool, 1)
            pool.wait_ge(s_pool, 1)
            nc.gpsimd.affine_select(out=ident[:], in_=ident[:], compare_op=ALU.not_equal, fill=1.0,
                                    base=0, pattern=[[-1, P]], channel_multiplier=1).then_inc(s_pool, 1)
            nc.gpsimd.iota(iota_e[:], pattern=[[1, NEST]], base=0, channel_multiplier=0,
                           allow_small_or_imprecise_dtypes=True).then_inc(s_pool, 1)

        @block.sync
        def _(sp):
            sp.dma_start(tok_i[:], x_txt).then_inc(loaded, 16)
            sp.dma_start(pos_raw[:], pos[0:TXT, :]).then_inc(raw_loaded, 16)
            sp.dma_start(tab_raw[0:NEST, :], nest).then_inc(raw_loaded, 16)
            sp.dma_start(tab_raw[NEST:NEST + SEG, :], seg).then_inc(raw_loaded, 16)
            sp.dma_start(txt_wr[:], txt_w.rearrange("(a p) n -> p a n", p=P)).then_inc(raw_loaded, 16)
            sp.dma_start(gates_raw[0:2, :], group_w).then_inc(raw_loaded, 16)
            sp.dma_start(gates_raw[2:2 + E, :], expert_w).then_inc(raw_loaded, 16)
            sp.dma_start(in_raw[:, 0], sh_in.rearrange("(a p) n -> p a n", p=P)).then_inc(raw_loaded, 16)
            sp.dma_start(in_raw[:, 1], ex_in.rearrange("(a p) n -> p a n", p=P)).then_inc(raw_loaded, 16)
            sp.dma_start(out_raw[:, 0], sh_out).then_inc(raw_loaded, 16)
            sp.dma_start(out_raw[:, 1:], ex_out.rearrange("e p n -> p e n")).then_inc(raw_loaded, 16)
            sp.dma_start(attn_raw[:], attn_w.rearrange("a p n -> p a n")).then_inc(raw_loaded, 16)
            sp.dma_start(wo[:], head_w.rearrange("(a p) n -> p a n", p=P)).then_inc(raw_loaded, 16)
            sp.dma_start(ln_cols[:, 0:1], ln_scale.rearrange("(p a) -> p a", a=1)).then_inc(raw_loaded, 16)
            sp.dma_start(ln_cols[:, 1:2], ln_bias.rearrange("(p a) -> p a", a=1)).then_inc(raw_loaded, 16)
            sp.dma_start(gate_b[:, 0:2], group_b.rearrange("(a n) -> a n", a=1).broadcast_to((P, 2))).then_inc(raw_loaded, 16)
            sp.dma_start(gate_b[:, 2:2 + E], expert_b.rearrange("(a n) -> a n", a=1).broadcast_to((P, E))).then_inc(raw_loaded, 16)
            sp.wait_ge(zeroed, N_ZEROED)
            for q in range(4):
                sp.dma_start(bias_rows[32 * q:32 * q + E, q, :], ex_out_b).then_inc(raw_loaded, 16)
                sp.dma_start(bias_rows[32 * q + E:32 * q + E + 1, q, :],
                             sh_out_b.rearrange("(a n) -> a n", a=1)).then_inc(raw_loaded, 16)
                sp.dma_start(tok_blocks[32 * q:32 * q + F, q, :], tok_w).then_inc(raw_loaded, 16)
            sp.wait_ge(s_text, 1)
            sp.dma_start(text_dram.rearrange("b t d -> t b d"), text_h[:]).then_inc(s_stored, 16)
            sp.wait_ge(s_stored, 16)
            sp.wait_ge(raw_loaded, 16 * 28)

        in_turns = [(in_raw[:, w, a, :], P) for w in range(2) for a in range(4)]
        out_turns = [(out_raw[:, e, k * P:(k + 1) * P], P) for e in range(1 + E) for k in range(KC)]
        turns = in_turns + out_turns
        groups = [turns[n:n + 4] for n in range(0, len(turns), 4)]
        NG = len(groups)

        @block.tensor
        def _(pe):
            pe.wait_ge(raw_loaded, 16 * 28)
            pe.wait_ge(s_pool, 2)
            nc.tensor.transpose(work[:, 0, 0:2 + E], gates_raw[:], ident[0:2 + E, 0:2 + E])
            nc.tensor.transpose(work[:, 0, 16:16 + TXT], pos_raw[:], ident[0:TXT, 0:TXT])
            nc.tensor.transpose(work[:, 0, 128:128 + NEST + SEG], tab_raw[:],
                                ident[0:NEST + SEG, 0:NEST + SEG]).then_inc(s_turned, 1)
            pe.wait_ge(s_dve, 1)
            nc.tensor.transpose(work[0:TXT, 1, 0:B], idx[:, 0, :], ident[0:B, 0:B])
            nc.tensor.transpose(work[0:TXT, 1, B:2 * B], idx[:, 1, :], ident[0:B, 0:B]).then_inc(s_turned, 1)
            pe.wait_ge(s_taken, 1)
            nc.tensor.matmul(work[0:TXT, 2, 0:D], pos_t[:], txt_wr[:, 0, :], start=True, stop=True)
            nc.tensor.matmul(work[0:NEST + SEG, 2, D:2 * D], tabs_n[:], txt_wr[:, 1, :], start=True, stop=False)
            nc.tensor.matmul(work[0:NEST + SEG, 2, D:2 * D], tabs_s[:], txt_wr[:, 2, :],
                             start=False, stop=True).then_inc(s_turned, 1)
            pe.wait_ge(s_taken, 3)
            for g in range(4):
                for i in range(4):
                    last = nc.tensor.transpose(scores[0:NEST + SEG, g // 2, g % 2, i * TXT:(i + 1) * TXT],
                                               onehot[:, 4 * g + i, :], ident[0:TXT, 0:TXT])
                last.then_inc(s_turned, 1)
            for g in range(4):
                pe.wait_ge(s_taken, 4 + g)
                for i in range(4):
                    last = nc.tensor.matmul(scores[0:TXT, g // 2, g % 2, i * D:(i + 1) * D],
                                            hot_t[:, 4 * g + i, :], rows24[:], start=True, stop=True)
                last.then_inc(s_turned, 1)
            for g, group in enumerate(groups):
                if g >= LANES:
                    pe.wait_ge(s_taken, 8 + g - LANES)
                for i, (src, _) in enumerate(group):
                    last = nc.tensor.transpose(work[:, g % LANES, i * P:(i + 1) * P], src, ident[:])
                last.then_inc(s_turned, 1)

        @block.scalar
        def _(act):
            act.wait_ge(raw_loaded, 16 * 28)
            v = attn_raw[:].rearrange("p (h w) n -> p w h n", w=3)
            nc.scalar.copy(wqk_hi[:, 0], v[:, 0])
            nc.scalar.copy(wqk_hi[:, 1], v[:, 1])
            nc.scalar.copy(wv_hi[:].rearrange("p (h n) -> p h n", h=H), v[:, 2]).then_inc(s_hi, 1)

        @block.vector
        def _(dve):
            nc.vector.memset(bias_rows[:], 0.0).then_inc(zeroed, 1)
            nc.vector.memset(tok_blocks[:], 0.0).then_inc(zeroed, 1)
            nc.vector.memset(ones[:], 1.0).then_inc(zeroed, 1)
            nc.vector.memset(one_b[:], 1.0).then_inc(zeroed, 1)
            done = [0]
            chain = s_chain

            def then(ins):
                done[0] += 1
                ins.then_inc(chain, 1)
                dve.wait_ge(chain, done[0])

            dve.wait_ge(loaded, 16)
            dve.wait_ge(zeroed, N_ZEROED)
            then(nc.vector.tensor_copy(tok[:], tok_i[:]))
            for mark, codes in ((opens, (40.0, 123.0, 91.0)), (closes, (41.0, 125.0, 93.0))):
                then(nc.vector.tensor_scalar(mark[:], tok[:], codes[0], None, ALU.is_equal))
                for code in codes[1:]:
                    then(nc.vector.scalar_tensor_tensor(out=mark[:], in0=tok[:], scalar=code, in1=mark[:],
                                                        op0=ALU.is_equal, op1=ALU.add))
            then(nc.vector.tensor_tensor(opens[:], opens[:], closes[:], ALU.subtract))
            then(nc.vector.tensor_tensor_scan(runs[:], one_b[:], opens[:], 0.0, ALU.mult, ALU.add))
            then(nc.vector.tensor_tensor_scan(low[:], runs[:], runs[:], 0.0, ALU.min, ALU.min))
            then(nc.vector.tensor_tensor(opens[:], runs[:], low[:], ALU.subtract))
            then(nc.vector.tensor_scalar(idx[:, 0, :], opens[:], 0.0, float(NEST - 1), ALU.max, ALU.min))
            then(nc.vector.tensor_scalar(closes[:], tok[:], 39990.0, None, ALU.is_gt))
            then(nc.vector.tensor_tensor_scan(runs[:], one_b[:], closes[:], 0.0, ALU.mult, ALU.add))
            then(nc.vector.tensor_copy(low[:], runs[:]))
            for m in range(8, TXT + 1, 8):
                then(nc.vector.tensor_scalar(closes[:], runs[:], float(m), -8.0, ALU.is_ge, ALU.mult))
                then(nc.vector.tensor_tensor(low[:], low[:], closes[:], ALU.add))
            nc.vector.tensor_copy(idx[:, 1, :], low[:]).then_inc(s_dve, 1)
            dve.wait_ge(s_turned, 1)
            nc.vector.tensor_copy(gate_w[:], work[:, 0, 0:2 + E])
            nc.vector.tensor_copy(pos_t[:], work[:, 0, 16:16 + TXT])
            nc.vector.memset(tabs_n[:, NEST:], 0.0)
            nc.vector.memset(tabs_s[:, 0:NEST], 0.0)
            nc.vector.tensor_copy(tabs_n[:, 0:NEST], work[:, 0, 128:128 + NEST])
            nc.vector.tensor_copy(tabs_s[:, NEST:], work[:, 0, 128 + NEST:128 + NEST + SEG]).then_inc(s_taken, 1)
            dve.wait_ge(s_turned, 2)
            then(nc.vector.tensor_copy(idx_t[:].rearrange("p a b -> p (a b)"), work[0:TXT, 1, 0:2 * B]))
            dve.wait_ge(s_pool, 3)
            for w, (a, n) in enumerate(((0, NEST), (NEST, SEG))):
                last = nc.vector.tensor_tensor(onehot[:, :, a:a + n],
                                               idx_t[:, w, :].unsqueeze(2).broadcast_to((TXT, B, n)),
                                               iota_e[:, 0:n].unsqueeze(1).broadcast_to((TXT, B, n)), ALU.is_equal)
            last.then_inc(s_taken, 1)
            dve.wait_ge(s_turned, 3)
            then(nc.vector.tensor_copy(base[:], work[0:TXT, 2, 0:D]))
            nc.vector.tensor_copy(rows24[:], work[0:NEST + SEG, 2, D:2 * D]).then_inc(s_taken, 1)
            for g in range(4):
                dve.wait_ge(s_turned, 4 + g)
                nc.vector.tensor_copy(hot_t[:, 4 * g:4 * g + 4, :].rearrange("p a b -> p (a b)"),
                                      scores[0:NEST + SEG, g // 2, g % 2, 0:4 * TXT]).then_inc(s_taken, 1)
            for g in range(4):
                dve.wait_ge(s_turned, 8 + g)
                ins = nc.vector.tensor_tensor(text_h[:, 4 * g:4 * g + 4, :],
                                              scores[0:TXT, g // 2, g % 2, :].rearrange("p (a b) -> p a b", a=4),
                                              base[:].unsqueeze(1).broadcast_to((TXT, 4, D)), ALU.add)
                if g == 3:
                    ins.then_inc(s_text, 1)
            for g, group in enumerate(groups):
                dve.wait_ge(s_turned, 12 + g)
                n = len(group) * P
                then(nc.vector.tensor_copy(turned[:, g % 4, 0:n], work[:, g % LANES, 0:n]))
                if g < 2:
                    then(nc.vector.tensor_copy(up_hi[:, g].rearrange("p a n -> p (a n)"), turned[:, g % 4, :]))
                    nc.vector.tensor_tensor(up_lo[:, g].rearrange("p a n -> p (a n)"), turned[:, g % 4, :],
                                            up_hi[:, g].rearrange("p a n -> p (a n)"), ALU.subtract).then_inc(s_taken, 1)
                    continue
                for i in range(len(group)):
                    m = 4 * (g - 2) + i
                    e, k = m // KC, m % KC
                    src = turned[:, g % 4, i * P:(i + 1) * P]
                    if e == 0:
                        ins = nc.vector.tensor_copy(down_sh[:, k, :], src)
                    else:
                        hi, lo = down_hi[:, k, (e - 1) * D:e * D], down_lo[:, k, (e - 1) * D:e * D]
                        then(nc.vector.tensor_copy(hi, src))
                        ins = nc.vector.tensor_tensor(lo, src, hi, ALU.subtract)
                    if i < len(group) - 1:
                        then(ins)
                ins.then_inc(s_taken, 1)
            dve.wait_ge(s_hi, 1)
            v = attn_raw[:].rearrange("p (h w) n -> p w h n", w=3)
            nc.vector.tensor_tensor(wqk_lo[:, 0], v[:, 0], wqk_hi[:, 0], ALU.subtract)
            nc.vector.tensor_tensor(wqk_lo[:, 1], v[:, 1], wqk_hi[:, 1], ALU.subtract)
            nc.vector.tensor_tensor(wv_lo[:].rearrange("p (h n) -> p h n", h=H), v[:, 2],
                                    wv_hi[:].rearrange("p (h n) -> p h n", h=H), ALU.subtract)

    yt_hi = sb(ctx, "yt_hi", [P, TW], F32R)
    yt_lo = sb(ctx, "yt_lo", [P, TW], F32R)
    q_a = [[sb(ctx, f"q_a{r}{i}", [P, TP], F32R) for i in range(2)] for r in range(2)]
    k_a = [[sb(ctx, f"k_a{r}{i}", [P, TP], F32R) for i in range(2)] for r in range(2)]
    q_b = [[sb(ctx, f"q_b{r}{i}", [P, TP], F32R) for i in range(2)] for r in range(2)]
    k_b = [[sb(ctx, f"k_b{r}{i}", [P, TP], F32R) for i in range(2)] for r in range(2)]
    values = sb(ctx, "values", [P, NT, H * DH])
    probs = sb(ctx, "probs", [P, NP, 2, CHUNK])
    sums = sb(ctx, "sums", [P, 2, 2, CHUNK])
    heads_t = sb(ctx, "heads_t", [P, PAIRS, TW])
    part_max = sb(ctx, "part_max", [P, 2 * NT, NC])
    neg_max = sb(ctx, "neg_max", [P, 2 * NT])
    max_rows = sb(ctx, "max_rows", [2 * NT, P], F32R)
    h_in = sb(ctx, "h_in", [P, NT, D])
    h_out = sb(ctx, "h_out", [P, NT, D])
    normed = sb(ctx, "normed", [P, NT * D])
    x_t = normed[:, 0:2 * P]
    counts = sb(ctx, "counts", [P, 12, 32])
    counts_t = sb(ctx, "counts_t", [P, 3 * P])
    flat_hi = sb(ctx, "flat_hi", [P, 2, GW], F32R)
    flat_lo = sb(ctx, "flat_lo", [P, 2, GW], F32R)
    hid = sb(ctx, "hid", [P, 2, KC, GW])
    hid_hi = sb(ctx, "hid_hi", [P, KC, GW], F32R)
    hid_lo = sb(ctx, "hid_lo", [P, KC, GW], F32R)
    stats = sb(ctx, "stats", [P, NT, 6])
    mean2 = sb(ctx, "mean2", [P, NT])
    neg_mean = [sb(ctx, f"neg_mean{n}", [P, NT]) for n in range(2)]
    mdiff = sb(ctx, "mdiff", [P, NT])
    msq = sb(ctx, "msq", [P, NT])
    var = [sb(ctx, f"var_{n}", [P, NT]) for n in range(2)]
    minus_half = sb(ctx, "minus_half", [P, NT])
    rstd = [sb(ctx, f"rstd_{n}", [P, NT]) for n in range(2)]
    shift = [sb(ctx, f"shift_{n}", [P, NT]) for n in range(2)]
    logits = sb(ctx, "logits", [P, NT, 2 + E])
    g_on = sb(ctx, "g_on", [P, 2, NT])
    e_sel = sb(ctx, "e_sel", [P, NT, EG])
    e_tmp = sb(ctx, "e_tmp", [P, NT, EG])
    e_exp = sb(ctx, "e_exp", [P, NT, EG])
    e_max = sb(ctx, "e_max", [P, NT])
    rank = sb(ctx, "rank", [P, NT, EG])
    beats = sb(ctx, "beats", [P, 3, NT, 3])
    four = sb(ctx, "four", [P, EG])
    den = sb(ctx, "den", [P, 2, NT])
    comb = sb(ctx, "comb", [P, NT, E])

    filled = [sem(f"work_filled{k}") for k in range(LANES)]
    drained = [sem(f"work_drained{k}") for k in range(LANES)]
    x_loaded = sem("x_loaded")
    seeded = sem("seeded")
    resid_stored = sem("resid_stored")
    resid_loaded = sem("resid_loaded")
    out_stored = sem("out_stored")
    max_loaded = sem("max_loaded")
    scores_ready = sem("scores_ready")
    probs_ready = sem("probs_ready")
    probs_used = sem("probs_used")
    sums_done = sem("sums_done")
    heads_out = sem("heads_out")
    heads_scaled = sem("heads_scaled")
    qk_hi = sem("qk_hi")
    max_ready = sem("max_ready")
    yt_hi_ready = sem("yt_hi_ready")
    var_ready = [sem(f"var_ready{n}") for n in range(2)]
    rstd_ready = [sem(f"rstd_ready{n}") for n in range(2)]
    shift_ready = [sem(f"shift_ready{n}") for n in range(2)]
    norm_ready = [sem(f"norm_ready{n}") for n in range(2)]
    flat_split = sem("flat_split")
    sel_ready = sem("sel_ready")
    sel_exp = sem("sel_exp")
    counted = sem("counted")
    tanh_ready = sem("tanh_ready")
    hid_split = sem("hid_split")
    sp_passed = sem("sp_passed")
    prepared = sem("prepared")

    last_max = [maxima(p)[0][-1] for p in range(PAIRS)]
    max_needs = {}
    for p in range(PAIRS):
        max_needs.update(maxima(p)[1])

    pro = Segment(False, False, True, [0] * LANES)
    first = Segment(True, False, True, pro.after(1))
    loop = Segment(True, True, True, first.after(1))
    last = Segment(True, True, False, loop.after(B - 2))
    epi = Segment(False, True, False, last.after(1))

    def wait(eng, s, v):
        if not isinstance(v, int) or v > 0:
            eng.wait_ge(s, v)

    def wait_filled(eng, seg, it, u):
        wait(eng, filled[seg.bank[u]], seg.value(it, u))

    def wait_drained(eng, seg, it, *units):
        for k in range(LANES):
            of_bank = [u for u in units if seg.bank[u] == k]
            if of_bank:
                wait(eng, drained[k], seg.value(it, max(of_bank, key=seg.order.get)))

    def wait_bank(eng, seg, it, u, *needed):
        wait(eng, drained[seg.bank[u]], seg.value(it, u) - 1)
        wait_drained(eng, seg, it, *[n for n in needed if seg.bank[n] != seg.bank[u]])

    def run(eng, step):
        def iteration(seg, it, b):
            for s in range(ALL):
                step(seg, it, b, s)
        iteration(pro, 0, -1)
        iteration(first, 0, 0)
        with eng.Fori(1, B - 1) as b:
            iteration(loop, b - 1, b)
        iteration(last, 0, B - 1)
        iteration(epi, 0, B)

    def cut(s):
        return s // STEPS, s % STEPS // NT, s % NT

    def summed(s):
        return (NT - 1) * (s // NT) + max(s % NT, 1)

    block = ctx.enter_context(nc.Block())

    @block.tensor
    def _(pe):
        def needs(u):
            if u[0] == "qk" and u[1:] == (0, "k", 0):
                return [("turn1", g) for g in range(3)]
            if u[0] == "max":
                return max_needs.get(u, [])
            if u[0] == "gate":
                return [("turn2", g) for g in range(3)]
            if u[0] == "shared":
                return [("up", u[1] // 3, 0, k, 1) for k in range(KC)] + [("count",)]
            if u[0] == "embed":
                return [("turnx",)]
            return []

        def unit(seg, it, b, u):
            k, kind = seg.bank[u], u[0]
            w = work[:, k, :]
            wait_bank(pe, seg, it, u, *needs(u))
            if kind == "v":
                j = u[1]
                for n, (y, wv) in enumerate(((yt_hi, wv_hi), (yt_lo, wv_hi), (yt_hi, wv_lo))):
                    mm = nc.tensor.matmul(w, y[:, j * P:(j + 1) * P], wv[:], start=(n == 0), stop=(n == 2))
            elif kind == "qk":
                _, p, what, c = u
                m = "qk".index(what)
                c0, cw = CHUNKS[c]
                for n, (wt, y) in enumerate(((wqk_hi, yt_hi), (wqk_hi, yt_lo), (wqk_lo, yt_hi))):
                    mm = nc.tensor.matmul(w[:, 0:cw], wt[:, m, 2 * p:2 * p + 2, :].rearrange("p a n -> p (a n)"),
                                          y[:, c0:c0 + cw], start=(n == 0), stop=(n == 2))
            elif kind == "max":
                _, p, i, j, c = u
                c0, cw = CHUNKS[c]
                n = queries(j)
                mm = nc.tensor.matmul(w[0:n, 0:cw], q_a[p % 2][i][:, j * P:j * P + n],
                                      k_a[p % 2][i][:, c0:c0 + cw], start=True, stop=True)
            elif kind == "maxrow":
                pe.wait_ge(max_ready, PAIRS * b + (u[1] - 1) % PAIRS + 2)
                mm = nc.tensor.transpose(w[0:2 * NT, 0:P], neg_max[:], ident[:])
            elif kind == "sum":
                q = u[1]
                bb = b - 1 if q == PAIRS * NC - 1 else b
                pe.wait_ge(sums_done, (NT - 1) * (PAIRS * NC * bb + q + 1))
                cw = CHUNKS[q % NC][1]
                for i in range(2):
                    mm = nc.tensor.matmul(w[64 * i:64 * i + 64, 0:cw], ones[:], sums[:, q % 2, i, 0:cw],
                                          start=True, stop=True)
            elif kind == "proj":
                j = u[1]
                if j == 0:
                    pe.wait_ge(heads_scaled, PAIRS * NC * b)
                for p in range(PAIRS):
                    mm = nc.tensor.matmul(w[:, 0:D], heads_t[:, p, j * P:(j + 1) * P], wo[:, p, :],
                                          start=(p == 0), stop=(p == PAIRS - 1))
            elif kind in ("turn1", "turn2"):
                g, n = u[1], int(kind == "turn2")
                item = b - 1 if n else b + 1
                pe.wait_ge(norm_ready[n], NT * item + 3 * g + 3)
                for j in range(3):
                    mm = nc.tensor.transpose(w[:, j * P:(j + 1) * P],
                                             normed[:, (3 * g + j) * P:(3 * g + j + 1) * P], ident[:])
            elif kind == "gate":
                for j in range(NT):
                    mm = nc.tensor.matmul(w[:, j * (2 + E):(j + 1) * (2 + E)], normed[:, j * P:(j + 1) * P],
                                          gate_w[:], start=True, stop=True)
            elif kind == "count":
                pe.wait_ge(counted, b)
                for g in range(3):
                    mm = nc.tensor.transpose(w[:, g * P:(g + 1) * P],
                                             counts[:, 4 * g:4 * g + 4, :].rearrange("p a n -> p (a n)"), ident[:])
            elif kind == "up":
                _, c, path, k2, half = u
                pe.wait_ge(flat_split, 3 * (b - 1) + c + 1)
                m = 2 * half + k2
                for n, (wt, y) in enumerate(((up_hi, flat_hi), (up_hi, flat_lo), (up_lo, flat_hi))):
                    mm = nc.tensor.matmul(w[:, 0:GW], wt[:, path, m, :], y[:, c % 2, :],
                                          start=(n == 0), stop=(n == 2))
            elif kind == "shared":
                t = u[1]
                for k2 in range(KC):
                    nc.tensor.matmul(w[:, 0:D], hid[:, 0, k2, t % 3 * P:(t % 3 + 1) * P], down_sh[:, k2, :],
                                     start=(k2 == 0), stop=False)
                mm = nc.tensor.matmul(w[:, 0:D], counts_t[:, t // 4 * P:(t // 4 + 1) * P], bias_rows[:, t % 4, :],
                                      start=False, stop=True)
            elif kind == "expert":
                _, t, g = u
                pe.wait_ge(hid_split, 3 * KC * (b - 1) + KC * (t // 3 + 1))
                cols = slice(t % 3 * P, (t % 3 + 1) * P)
                ops = [(k2, h, wt) for k2 in range(KC)
                       for h, wt in ((hid_hi, down_hi), (hid_lo, down_hi), (hid_hi, down_lo))]
                for n, (k2, h, wt) in enumerate(ops):
                    mm = nc.tensor.matmul(w, h[:, k2, cols], wt[:, k2, g * EG * D:(g + 1) * EG * D],
                                          start=(n == 0), stop=(n == len(ops) - 1))
            elif kind == "turnx":
                pe.wait_ge(x_loaded, 16 * (b + 2))
                if seg.post:
                    pe.wait_ge(flat_split, 3 * b)
                for g in range(2):
                    mm = nc.tensor.transpose(w[:, g * P:(g + 1) * P],
                                             counts[:, 4 * g:4 * g + 4, :].rearrange("p a n -> p (a n)"), ident[:])
            elif kind == "embed":
                g = u[1]
                mm = nc.tensor.matmul(w, x_t[:, g * P:(g + 1) * P], tok_blocks[:].rearrange("p a n -> p (a n)"),
                                      start=True, stop=True)
            mm.then_inc(filled[k], 1)

        def score(seg, b, s):
            p, c, t = cut(s)
            if s % STEPS == 0:
                pe.wait_ge(max_loaded, 64 * (PAIRS * b + p + 1))
            wait(pe, probs_ready, ALL * b + s - 1)
            c0, cw = CHUNKS[c]
            n = rows(t)
            for i in range(2):
                o = scores[0:n, s % 2, i, 0:cw]
                nc.tensor.matmul(o, k_a[p % 2][i][:, t * P:t * P + n], q_a[p % 2][i][:, c0:c0 + cw],
                                 start=True, stop=False)
                mm = nc.tensor.matmul(o, k_b[p % 2][i][:, t * P:t * P + n], q_b[p % 2][i][:, c0:c0 + cw],
                                      start=False, stop=True)
            mm.then_inc(scores_ready, 1)

        def weigh(seg, it, b, s):
            p, c, t = cut(s)
            pe.wait_ge(probs_ready, ALL * b + s + 1)
            if s < NT:
                wait_drained(pe, seg, it, ("v", t))
            if t == 0:
                wait(pe, heads_out, PAIRS * NC * b + s // NT)
            cw, n = CHUNKS[c][1], rows(t)
            for i in range(2):
                h = 2 * p + i
                mm = nc.tensor.matmul(o_ps[64 * i:64 * i + 64, 0:cw], values[0:n, t, h * DH:(h + 1) * DH],
                                      probs[0:n, s % NP, i, 0:cw], start=(t == 0), stop=(t == NT - 1))
            mm.then_inc(probs_used, 1)

        def step(seg, it, b, s):
            units = seg.at[s]
            if seg.attn:
                score(seg, b, s)
                if s > 0:
                    early = len(units) // 2 if s % NT else 0
                    for u in units[:early]:
                        unit(seg, it, b, u)
                    units = units[early:]
                    weigh(seg, it, b, s - 1)
            for u in units:
                unit(seg, it, b, u)
            if seg.attn and s == ALL - 1:
                weigh(seg, it, b, s)

        pe.wait_ge(prepared, 1)
        run(pe, step)

    @block.scalar
    def _(act):
        def unit(seg, it, b, u):
            k, kind = seg.bank[u], u[0]
            w = work[:, k, :]
            if kind not in ("v", "qk", "sum", "turn1", "turn2", "count", "up", "turnx") or (kind == "up" and u[4]):
                return
            wait_filled(act, seg, it, u)
            if kind == "v":
                wait(act, probs_used, ALL * b)
                nc.scalar.copy(values[:, u[1], :], w).then_inc(drained[k], 1)
            elif kind == "qk":
                _, p, what, c = u
                c0, cw = CHUNKS[c]
                for i in range(2):
                    src = w[64 * i:64 * i + 64, 0:cw]
                    a, z = (k_a, k_a) if what == "k" else (q_a, q_b)
                    nc.scalar.copy(a[p % 2][i][0:64, c0:c0 + cw], src)
                    o = 64 if what == "k" else 0
                    ins = nc.scalar.copy(z[p % 2][i][o:o + 64, c0:c0 + cw], src)
                ins.then_inc(qk_hi, 1)
            elif kind == "sum":
                q = u[1]
                cw = CHUNKS[q % NC][1]
                nc.scalar.copy(sums[:, q % 2, 0, 0:cw], w[:, 0:cw]).then_inc(drained[k], 1)
            elif kind == "turn1":
                g = u[1]
                nc.scalar.copy(yt_hi[:, g * GW:(g + 1) * GW], w[:, 0:GW]).then_inc(yt_hi_ready, 1)
            elif kind == "turn2":
                g = u[1]
                nc.scalar.activation(normed[:, g * GW:(g + 1) * GW], w[:, 0:GW], ACT.Identity,
                                     bias=ln_cols[:, 1:2], scale=ln_cols[:, 0:1]).then_inc(drained[k], 1)
            elif kind == "count":
                nc.scalar.copy(counts_t[:], w[:, 0:3 * P]).then_inc(drained[k], 1)
            elif kind == "turnx":
                nc.scalar.copy(x_t, w[:, 0:2 * P]).then_inc(drained[k], 1)
            elif kind == "up":
                _, c, path, k2, half = u
                nc.scalar.activation(hid[:, path, k2, :], w[:, 0:GW], ACT.Tanh, scale=0.5).then_inc(tanh_ready, 1)

        def normalise(n, item, src, g):
            act.wait_ge(shift_ready[n], item + 1)
            for j in range(3 * g, 3 * g + 3):
                nc.scalar.activation(normed[:, j * D:(j + 1) * D], src[:, j, :], ACT.Identity,
                                     bias=shift[n][:, j:j + 1], scale=rstd[n][:, j:j + 1]).then_inc(norm_ready[n], 1)

        def heads(seg, it, b, q):
            act.wait_ge(probs_used, ALL * b + NT * (q + 1))
            if q < NC and seg.post:
                wait_filled(act, seg, it, ("proj", 3 * q + 2))
            c0, cw = CHUNKS[q % NC]
            nc.scalar.copy(heads_t[:, q // NC, c0:c0 + cw], o_ps[:, 0:cw]).then_inc(heads_out, 1)

        def step(seg, it, b, s):
            if seg.attn:
                p, c, t = cut(s)
                act.wait_ge(scores_ready, ALL * b + s + 1)
                wait(act, probs_used, ALL * b + s - NP + 1)
                if not isinstance(b, int) or b > 0 or s >= NP:
                    wait(act, sums_done, (NT - 1) * PAIRS * NC * b + summed(s - NP))
                cw, n = CHUNKS[c][1], rows(t)
                nc.scalar.activation(probs[0:n, s % NP, :, 0:cw], scores[0:n, s % 2, :, 0:cw], ACT.Exp,
                                     scale=DH ** -0.5).then_inc(probs_ready, 1)
                if t == 0 and s > 0:
                    heads(seg, it, b, s // NT - 1)
            if seg.post and TURN - 2 <= s <= TURN:
                normalise(1, b - 1, h_out, s - TURN + 2)
            if seg.prep and EMBED + 5 <= s <= EMBED + 7:
                normalise(0, b + 1, h_in, s - EMBED - 5)
            if seg.post and s == GATE + 2:
                act.wait_ge(sel_ready, b)
                nc.scalar.activation(e_exp[:], e_sel[:], ACT.Exp).then_inc(sel_exp, 1)
            for u in seg.at[s]:
                unit(seg, it, b, u)
            if seg.attn and s == ALL - 1:
                heads(seg, it, b, PAIRS * NC - 1)

        act.wait_ge(prepared, 1)
        run(act, step)

    @block.vector
    def _(dve):
        done = [0]

        def then(ins):
            done[0] += 1
            ins.then_inc(s_chain, 1)
            dve.wait_ge(s_chain, done[0])

        def unit(seg, it, b, u):
            k, kind = seg.bank[u], u[0]
            w = work[:, k, :]
            if kind in ("v", "sum", "turn2", "count", "turnx"):
                return
            wait_filled(dve, seg, it, u)
            if kind == "qk":
                _, p, what, c = u
                c0, cw = CHUNKS[c]
                n = 6 * (PAIRS * b + (p - 1) % PAIRS + 1) + 2 * c + "kq".index(what) + 1
                dve.wait_ge(qk_hi, n)
                for i in range(2):
                    src = w[64 * i:64 * i + 64, 0:cw]
                    if what == "k":
                        ins = nc.vector.tensor_tensor(k_b[p % 2][i][0:64, c0:c0 + cw], src,
                                                      k_a[p % 2][i][0:64, c0:c0 + cw], ALU.subtract)
                    else:
                        ins = nc.vector.tensor_tensor(q_a[p % 2][i][64:128, c0:c0 + cw], src,
                                                      q_b[p % 2][i][0:64, c0:c0 + cw], ALU.subtract)
                ins.then_inc(drained[k], 1)
            elif kind == "max":
                _, p, i, j, c = u
                n = queries(j)
                keys = min(CHUNKS[c][1], T - CHUNKS[c][0])
                nc.vector.tensor_reduce(part_max[0:n, i * NT + j, c:c + 1], w[0:n, 0:keys], AX.X,
                                        ALU.max).then_inc(drained[k], 1)
                if u == last_max[p]:
                    wait_drained(dve, seg, it, u)
                    nc.vector.tensor_reduce(neg_max[:], part_max[:], AX.X, ALU.max, negate=True).then_inc(max_ready, 1)
            elif kind == "maxrow":
                wait(dve, max_loaded, 64 * (PAIRS * b + (u[1] - 1) % PAIRS + 1))
                nc.vector.tensor_copy(max_rows[:], w[0:2 * NT, 0:P]).then_inc(drained[k], 1)
            elif kind == "proj":
                j = u[1]
                dve.wait_ge(resid_loaded, 16 * b)
                nc.vector.tensor_tensor(h_out[:, j, :], w[:, 0:D], h_out[:, j, :], ALU.add).then_inc(drained[k], 1)
            elif kind == "turn1":
                g = u[1]
                dve.wait_ge(yt_hi_ready, 3 * (b + 1) + g + 1)
                cols = slice(g * GW, (g + 1) * GW)
                nc.vector.tensor_tensor(yt_lo[:, cols], w[:, 0:GW], yt_hi[:, cols], ALU.subtract).then_inc(drained[k], 1)
            elif kind == "gate":
                nc.vector.tensor_tensor(logits[:], w[:, 0:NT * (2 + E)].rearrange("p (a n) -> p a n", a=NT),
                                        gate_b[:].unsqueeze(1).broadcast_to((P, NT, 2 + E)),
                                        ALU.add).then_inc(drained[k], 1)
                wait_drained(dve, seg, it, u)
                choose_group()
            elif kind == "up":
                _, c, path, k2, half = u
                o = hid[:, path, k2, :]
                if half == 0:
                    dve.wait_ge(tanh_ready, 12 * (b - 1) + 4 * c + 2 * (1 - path) + k2 + 1)
                    nc.vector.scalar_tensor_tensor(out=o, in0=o, scalar=1.0, in1=w[:, 0:GW], op0=ALU.add,
                                                   op1=ALU.mult).then_inc(drained[k], 1)
                else:
                    wait_drained(dve, seg, it, ("up", c, path, k2, 0))
                    nc.vector.scalar_tensor_tensor(out=o, in0=o, scalar=0.5, in1=w[:, 0:GW], op0=ALU.mult,
                                                   op1=ALU.mult).then_inc(drained[k], 1)
                    if path == 1:
                        wait_drained(dve, seg, it, u)
                        then(nc.vector.tensor_copy(hid_hi[:, k2, :], o))
                        nc.vector.tensor_tensor(hid_lo[:, k2, :], o, hid_hi[:, k2, :],
                                                ALU.subtract).then_inc(hid_split, 1)
                if u == ("up", 0, 0, 1, 1):
                    split_flat(seg, it, 2)
            elif kind == "shared":
                t = u[1]
                nc.vector.tensor_tensor(h_out[:, t, :], w[:, 0:D], h_out[:, t, :], ALU.add).then_inc(drained[k], 1)
            elif kind == "expert":
                _, t, g = u
                wait_drained(dve, seg, it, ("expert", t, 0) if g else ("shared", t))
                o = h_out[:, t, :]
                for e in range(EG):
                    ins = nc.vector.scalar_tensor_tensor(
                        out=o, in0=w[:, e * D:(e + 1) * D], scalar=comb[:, t, g * EG + e:g * EG + e + 1],
                        in1=o, op0=ALU.mult, op1=ALU.add)
                    if e < EG - 1:
                        then(ins)
                ins.then_inc(drained[k], 1)
            elif kind == "embed":
                g = u[1]
                wait(dve, seeded, 32 * (b + 2))
                o = h_in[:, 4 * g:4 * g + 4, :].rearrange("p a n -> p (a n)")
                nc.vector.tensor_tensor(o, w, o, ALU.add).then_inc(drained[k], 1)

        def divide(seg, it, b, q, part):
            n = PAIRS * NC * (b - 1 if q == PAIRS * NC - 1 else b) + q
            c0, cw = CHUNKS[q % NC]
            inverse = sums[:, q % 2, 0, :]
            if part == 0:
                wait_drained(dve, seg, it, ("sum", q))
                ins = nc.vector.reciprocal(inverse[:, 0:CHUNK // 2], inverse[:, 0:CHUNK // 2])
                then(ins)
            else:
                then(nc.vector.reciprocal(inverse[:, CHUNK // 2:cw], inverse[:, CHUNK // 2:cw]))
                dve.wait_ge(heads_out, n + 1)
                o = heads_t[:, q // NC, c0:c0 + cw]
                nc.vector.tensor_tensor(o, inverse[:, 0:cw], o, ALU.mult).then_inc(heads_scaled, 1)

        def split_flat(seg, it, c):
            wait_drained(dve, seg, it, ("turn2", c))
            src = normed[:, c * GW:(c + 1) * GW]
            then(nc.vector.tensor_copy(flat_hi[:, c % 2, :], src))
            nc.vector.tensor_tensor(flat_lo[:, c % 2, :], src, flat_hi[:, c % 2, :], ALU.subtract).then_inc(flat_split, 1)

        def statistics(src, tiles):
            for j in tiles:
                ins = nc.vector.bn_stats(stats[:, j, :], src[:, j, :])
            return ins

        def moments(n):
            nc.vector.tensor_tensor(mean2[:], stats[:, :, 1], stats[:, :, 4], ALU.add)
            nc.vector.tensor_tensor(msq[:], stats[:, :, 2], stats[:, :, 5], ALU.add)
            then(nc.vector.tensor_tensor(mdiff[:], stats[:, :, 1], stats[:, :, 4], ALU.subtract))
            nc.vector.tensor_scalar(neg_mean[n][:], mean2[:], -0.5, None, ALU.mult)
            then(nc.vector.scalar_tensor_tensor(out=mdiff[:], in0=mdiff[:], scalar=0.25, in1=mdiff[:],
                                                op0=ALU.mult, op1=ALU.mult))
            ins = nc.vector.scalar_tensor_tensor(out=var[n][:], in0=msq[:], scalar=1.0 / D, in1=mdiff[:],
                                                 op0=ALU.mult, op1=ALU.add)
            then(ins)
            scale, eps = (1.0 + EPS, EPS * EPS) if n else (1.0, EPS)
            nc.vector.tensor_scalar(var[n][:], var[n][:], scale, eps, ALU.mult, ALU.add).then_inc(var_ready[n], 1)

        def choose_group():
            nc.vector.tensor_tensor(g_on[:, 0, :], logits[:, :, 0], logits[:, :, 1], ALU.is_ge)
            then(nc.vector.tensor_tensor(g_on[:, 1, :], logits[:, :, 1], logits[:, :, 0], ALU.is_gt))
            for g, o in ((0, e_tmp), (1, e_sel)):
                ins = nc.vector.tensor_tensor(o[:], logits[:, :, 2 + g * EG:2 + (g + 1) * EG],
                                              g_on[:, g, :].unsqueeze(2).broadcast_to((P, NT, EG)), ALU.mult)
            then(ins)
            then(nc.vector.tensor_tensor(e_sel[:], e_sel[:], e_tmp[:], ALU.add))
            then(nc.vector.tensor_reduce(e_max[:], e_sel[:], AX.X, ALU.max))

        def rank_experts():
            for d in (1, 2, 3):
                nc.vector.tensor_tensor(beats[:, d - 1, :, 0:EG - d], e_sel[:, :, d:], e_sel[:, :, 0:EG - d], ALU.is_gt)
            then(nc.vector.tensor_copy(rank[:], four[:].unsqueeze(1).broadcast_to((P, NT, EG))))
            nc.vector.tensor_tensor(e_sel[:], e_sel[:], e_max[:].unsqueeze(2).broadcast_to((P, NT, EG)),
                                    ALU.subtract).then_inc(sel_ready, 1)
            for d in (1, 2, 3):
                m = beats[:, d - 1, :, 0:EG - d]
                then(nc.vector.tensor_tensor(rank[:, :, 0:EG - d], rank[:, :, 0:EG - d], m, ALU.add))
                then(nc.vector.tensor_tensor(rank[:, :, d:], rank[:, :, d:], m, ALU.subtract))
            then(nc.vector.tensor_scalar(rank[:], rank[:], 1.5, None, ALU.is_lt))

        def weights(b):
            for g in range(2):
                nc.vector.tensor_tensor(counts[:, 0:NT, g * EG:(g + 1) * EG], rank[:],
                                        g_on[:, g, :].unsqueeze(2).broadcast_to((P, NT, EG)), ALU.mult)
            nc.vector.memset(counts[:, 0:NT, E:E + 1], 1.0).then_inc(counted, 1)
            dve.wait_ge(sel_exp, b)
            nc.vector.tensor_tensor(e_tmp[:], e_exp[:], rank[:], ALU.mult)
            then(nc.vector.tensor_reduce(den[:, 0, :], e_exp[:], AX.X, ALU.add))
            then(nc.vector.tensor_reduce(den[:, 1, :], e_tmp[:], AX.X, ALU.add))
            then(nc.vector.scalar_tensor_tensor(out=den[:, 0, :], in0=den[:, 0, :], scalar=1e-8, in1=den[:, 1, :],
                                                op0=ALU.mult, op1=ALU.add))
            then(nc.vector.reciprocal(den[:, 1, :], den[:, 0, :]))
            then(nc.vector.tensor_tensor(e_tmp[:], e_tmp[:], den[:, 1, :].unsqueeze(2).broadcast_to((P, NT, EG)),
                                         ALU.mult))
            for g in range(2):
                ins = nc.vector.tensor_tensor(comb[:, :, g * EG:(g + 1) * EG], e_tmp[:],
                                              g_on[:, g, :].unsqueeze(2).broadcast_to((P, NT, EG)), ALU.mult)
            then(ins)

        def step(seg, it, b, s):
            if s == 0:
                if done[0]:
                    nc.vector.sem_clear(s_chain)
                done[0] = 0
            for u in seg.at[s]:
                unit(seg, it, b, u)
            for part in range(2):
                for u in seg.at[s - 1 - part] if s > part else []:
                    if u[0] == "sum":
                        divide(seg, it, b, u[1], part)
            if seg.post:
                for g in range(3):
                    if s == PROJ[3 * g + 2] + 1:
                        wait_drained(dve, seg, it, *[("proj", j) for j in range(3 * g, 3 * g + 3)])
                        then(statistics(h_out, range(3 * g, 3 * g + 3)))
                if s == STATS:
                    moments(1)
                if s in (TURN + 2, TURN + 3):
                    split_flat(seg, it, s - TURN - 2)
                if s == GATE + 1:
                    rank_experts()
                if s == WEIGHTS:
                    weights(b)
            if seg.prep and s == EMBED + 3:
                wait_drained(dve, seg, it, ("embed", 1))
                then(statistics(h_in, range(NT)))
                moments(0)

        nc.vector.sem_clear(s_chain)
        for r in range(2):
            for i in range(2):
                nc.vector.memset(q_b[r][i][64:128, :].bitcast(F32), 0.0)
                then(nc.vector.memset(k_b[r][i][64:128, :].bitcast(F32), 0.0))
                nc.vector.memset(k_b[r][i][64:65, :].bitcast(F32), 1.0)
        nc.vector.memset(heads_t[:], 0.0)
        nc.vector.memset(part_max[:], 0.0)
        nc.vector.memset(h_in[:], 0.0)
        nc.vector.memset(minus_half[:], -0.5)
        nc.vector.memset(four[:, 0:1], 0.0)
        nc.vector.memset(four[:, 1:2], 1.0)
        nc.vector.memset(four[:, 2:3], 2.0)
        nc.vector.memset(four[:, 3:4], 3.0)
        nc.vector.memset(counts[:], 0.0).then_inc(prepared, 1)
        dve.wait_ge(prepared, 1)
        run(dve, step)

    @block.gpsimd
    def _(pool):
        def root(n, item):
            pool.wait_ge(var_ready[n], item + 1)
            nc.gpsimd.tensor_tensor(rstd[n][:], var[n][:], minus_half[:], ALU.pow).then_inc(rstd_ready[n], 1)
            pool.wait_ge(rstd_ready[n], item + 1)
            nc.gpsimd.tensor_tensor(shift[n][:], neg_mean[n][:], rstd[n][:], ALU.mult).then_inc(shift_ready[n], 1)

        def step(seg, it, b, s):
            if seg.post and s == STATS:
                root(1, b - 1)
            if seg.prep and s == EMBED + 3:
                root(0, b + 1)
            if not seg.attn:
                return
            p, c, t = cut(s)
            if t == 0:
                return
            q = s // NT
            cw, n = CHUNKS[c][1], rows(t)
            pool.wait_ge(probs_ready, ALL * b + s + 1)
            acc = sums[0:n, q % 2, :, 0:cw]
            if t == 1:
                if not isinstance(b, int) or b > 0 or q >= 2:
                    pool.wait_ge(heads_scaled, PAIRS * NC * b + q - 1)
                nc.gpsimd.tensor_tensor(acc, probs[:, (s - 1) % NP, :, 0:cw], probs[:, s % NP, :, 0:cw],
                                        ALU.add).then_inc(sums_done, 1)
            else:
                pool.wait_ge(sums_done, (NT - 1) * (PAIRS * NC * b + q) + t - 1)
                nc.gpsimd.tensor_tensor(acc, acc, probs[0:n, s % NP, :, 0:cw], ALU.add).then_inc(sums_done, 1)

        pool.wait_ge(prepared, 1)
        run(pool, step)

    @block.sync
    def _(sp):
        def wait_then(sem_wait, *args):
            sem_wait(*args)
            sp.sem_inc(sp_passed, 1)

        x_rows = x.rearrange("b h w f -> b (h w) f").rearrange("b (p j) f -> b p j f", j=IMG)
        out_img = out[:, 0:HW, :].rearrange("b (p j) d -> b p j d", j=IMG)

        def seed(n):
            sp.dma_start(h_in[:, 0:IMG, :], pe_table.rearrange("(p j) d -> p j d", j=IMG)).then_inc(seeded, 16)
            sp.dma_start(h_in[0:TXT, IMG, :], text_dram[n]).then_inc(seeded, 16)

        def step(seg, it, b, s):
            if seg.post and s == 0:
                wait_then(sp.wait_ge, resid_stored, 16 * b)
                sp.dma_start(h_out[:].rearrange("p a n -> p (a n)"), resid_dram[b - 1]).then_inc(resid_loaded, 16)
            if seg.prep and s == 30:
                if seg.post:
                    wait_then(wait_drained, sp, seg, it, ("count",))
                sp.dma_start(counts[:, 0:IMG, 0:F], x_rows[b + 1]).then_inc(x_loaded, 16)
                wait_then(wait, sp, norm_ready[0], NT * (b + 1))
                seed(b + 1)
            if seg.prep and s == EMBED + 3:
                wait_then(wait_drained, sp, seg, it, ("embed", 1))
                sp.dma_start(resid_dram[b + 1], h_in[:].rearrange("p a n -> p (a n)")).then_inc(resid_stored, 16)
                wait_then(sp.wait_ge, resid_stored, 16 * (b + 2))
            for u in seg.at[s]:
                if u[0] == "maxrow":
                    wait_then(wait_drained, sp, seg, it, u)
                    for i in range(2):
                        row = q_b[u[1] % 2][i][64:65, :].bitcast(F32)
                        r = i * NT
                        sp.dma_start(row[:, 0:HW].rearrange("p (a n) -> p a n", a=IMG),
                                     max_rows[r:r + IMG, :].bitcast(F32)).then_inc(max_loaded, 16)
                        sp.dma_start(row[:, HW:TP], max_rows[r + IMG:r + NT, 0:TP - HW].bitcast(F32)).then_inc(max_loaded, 16)
            if seg.post and s == STORE:
                wait_then(wait_drained, sp, seg, it, ("expert", NT - 1, 1))
                sp.dma_start(out_img[b - 1], h_out[:, 0:IMG, :]).then_inc(out_stored, 16)
                sp.dma_start(out[b - 1, HW:T, :], h_out[0:TXT, IMG, :]).then_inc(out_stored, 16)
                wait_then(sp.wait_ge, out_stored, 32 * b)

        sp.wait_ge(prepared, 1)
        run(sp, step)

    ctx.close()


_INS = ['x', 'x_txt', 'L0_tok_W', 'L0_txt_pos_table', 'L0_txt_nest_table', 'L0_txt_seg_table', 'L0_txt_W',
        'L0_attn_kernel', 'L0_attn_head_kernel', 'L0_ffn_ln_scale', 'L0_ffn_ln_bias', 'L0_ffn_shared_in_w',
        'L0_ffn_shared_out_w', 'L0_ffn_shared_out_b', 'L0_ffn_expert_in_w', 'L0_ffn_expert_out_weight',
        'L0_ffn_expert_out_bias', 'L0_ffn_group_gate_w', 'L0_ffn_expert_gate_w', 'L0_ffn_group_bias',
        'L0_ffn_expert_bias']


def position_table():
    position = np.arange(HW, dtype=np.float32)[:, None]
    div_term = np.exp(np.arange(0, D, 2, dtype=np.float32) * np.float32(-np.log(10000.0) / D))
    table = np.zeros((HW, D), dtype=np.float32)
    table[:, 0::2] = np.sin(position * div_term)
    table[:, 1::2] = np.cos(position * div_term)
    return table


def kernel(**inputs):
    import concourse.bacc as bacc
    from concourse.bass_utils import run_bass_kernel_spmd

    nc = bacc.Bacc("TRN2", target_bir_lowering=False, num_devices=1)
    arrays, args = {}, []
    for name in _INS + ["pe_table"]:
        a = np.ascontiguousarray(inputs[name] if name in inputs else position_table())
        arrays[f"in_{name}_dram"] = a
        args.append(nc.dram_tensor(f"in_{name}_dram", a.shape, mybir.dt.from_np(a.dtype), kind="ExternalInput").ap())
    args.append(nc.dram_tensor("out_0_dram", (B, T, D), F32, kind="ExternalOutput").ap())
    fusion_kernel(nc, *args)
    r = run_bass_kernel_spmd(nc, [arrays], core_ids=[0])
    return r.results[0]["out_0_dram"]
```

```python
from contextlib import ExitStack

import numpy as np

import concourse.bass as bass
from concourse import mybir
from concourse.alu_op_type import AluOpType as ALU

F32 = mybir.dt.float32
F32R = mybir.dt.float32r
I32 = mybir.dt.int32
ACT = mybir.ActivationFunctionType
AX = mybir.AxisListType

P = 128
B, HW, F = 16, 1024, 29
TXT = 77
T = HW + TXT
TP = T + 1
IMG = HW // P
NT = IMG + 1
TW = NT * P
D = 128
H, DH = 8, 64
PAIRS = H // 2
CHUNK = 368
CHUNKS = [(0, CHUNK), (CHUNK, CHUNK), (2 * CHUNK, TP - 2 * CHUNK)]
NC = len(CHUNKS)
STEPS = NC * NT
ALL = PAIRS * STEPS
GW = 3 * P
E, EG, HID = 8, 4, 256
KC = HID // P
HALF = H * DH // 2
EPS = 1e-5
NEST, SEG = 16, 8
LANES = 4
SB = 3
NP = 3
PROJ = [4 + j for j in range(NT)]
STATS, TURN, GATE, WEIGHTS = 13, 18, 22, 25
EMBED = 59
MAXROW = 23
STORE = 102
PAUSE = ("pause",)
DIV = 4


def rows(t):
    return P if t < IMG else TXT


def queries(j):
    return P if j < IMG else TP - IMG * P


LOAD = {"v": (48, 0, 36), "qk": (48, 95, 130), "max": (16, 50, 0), "maxrow": (10, 50, 0), "sum": (65, 0, 36),
        "proj": (88, 20, 0), "turn1": (30, 50, 50), "turn2": (30, 0, 50), "gate": (60, 180, 0),
        "count": (30, 0, 50), "up": (48, 60, 20), "upx": (48, 60, 36), "shared": (66, 20, 0),
        "expert": (135, 155, 0), "turnx": (20, 0, 40), "embed": (90, 70, 0)}
STEP = (130, 0, 70)
JOB = {"invert": 63, "scale": 45, "split": 50, "statistics": 90, "moments": 130, "rank": 200, "weights": 200}
EVEN_MAX, EVEN_V, EVEN_POST = (0, 1, 0), (1, 0, 0), (1, 0.5, 0)


def projections(p):
    return [("qk", p, "kq"[n % 2], n // 2) for n in range(2 * NC)]


def maxima(p):
    units, first_need, seen = [], {}, set()
    for n in range(1, 2 * NC):
        c0, cw = CHUNKS[(n - 1) // 2]
        new = [("max", p, i, j, c) for i in range(2) for j in range(NT) for c in range(n // 2 + 1)
               if j * P + queries(j) <= c0 + cw and (i, j, c) not in seen]
        seen |= {u[2:] for u in new}
        first_need[new[0]] = projections(p)[0 if n == 1 else n:n + 1]
        units += new
    return units, first_need


def load(u):
    return LOAD["upx" if u[0] == "up" and u[2:] == (1, u[3], 1) else u[0]]


def plan(attn, post, prep):
    at = [[] for _ in range(ALL)]
    used = [list(STEP) if attn else [0, 0, 0] for _ in range(ALL)]

    def job(s, name):
        used[s][1] += JOB[name]

    def put(s, u):
        at[s].append(u)
        used[s] = [a + b for a, b in zip(used[s], load(u))]
        if u[0] == "sum":
            for part in range(DIV):
                job(s + 1 + part, "invert")
            job(s + 1 + DIV, "scale")
        if load(u) == LOAD["upx"]:
            job(s + 2, "split")

    def fill(units, first, last, weights):
        def weighted(loads):
            return sum(w * x for w, x in zip(weights, loads))

        def place(level):
            s, backlog, places = first, 0, []
            for u in units:
                while s <= last and (u == PAUSE or weighted(used[s]) + backlog >= level):
                    backlog = max(0, backlog + weighted(used[s]) - level)
                    s += 1
                    if u == PAUSE:
                        break
                if s > last:
                    return None
                if u != PAUSE:
                    places.append((s, u))
                    backlog += weighted(load(u))
            return places
        level = 50
        while place(level) is None:
            level += 2
        for s, u in place(level):
            put(s, u)

    if attn:
        for q in range(PAIRS * NC - 1):
            put(NT * (q + 1) + 2, ("sum", q))
    if post:
        put(1, ("sum", PAIRS * NC - 1))
        for j in range(NT):
            put(PROJ[j], ("proj", j))
        for g in range(3):
            job(PROJ[3 * g + 2] + 1, "statistics")
            put(TURN + g, ("turn2", g))
        job(STATS, "moments")
        put(GATE, ("gate",))
        job(GATE + 1, "rank")
        job(WEIGHTS, "weights")
        put(WEIGHTS + 2, ("count",))
    if prep:
        put(EMBED, ("turnx",))
        for g in range(2):
            put(EMBED + 1 + g, ("embed", g))
        for g in range(2):
            job(EMBED + 2 + g, "statistics")
        job(EMBED + 4, "moments")
        for g in range(3):
            put(EMBED + 11 + g, ("turn1", g))
    for p in range(PAIRS):
        if (attn and p < PAIRS - 1) or (prep and p == PAIRS - 1):
            nxt = (p + 1) % PAIRS
            for n, u in enumerate(projections(nxt)):
                put(STEPS * p + n, u)
            fill(maxima(nxt)[0], STEPS * p + 3, STEPS * p + MAXROW - 1, EVEN_MAX)
            put(STEPS * p + MAXROW, ("maxrow", nxt))
    if attn:
        fill([("v", 1, j) for j in range(NT)], MAXROW, 2 * STEPS - 3, EVEN_V)
    if prep:
        fill([("v", 0, j) for j in range(NT)], EMBED + 15, ALL - 2, EVEN_V)
    if post:
        units = []
        for c in range(3):
            for path in (1, 0):
                units += [("up", c, path, k, half) for k in range(KC) for half in range(2)] + [PAUSE]
            for t in range(3 * c, 3 * c + 3):
                units += [("shared", t), ("expert", t, 0), ("expert", t, 1)]
        fill(units, WEIGHTS + 3, STORE - 2, EVEN_POST)
    return at


class Segment:

    def __init__(self, attn, post, prep, before):
        self.attn, self.post, self.prep = attn, post, prep
        self.ends = post
        self.at = plan(attn, post, prep)
        self.before = before
        self.uses = [0] * LANES
        self.bank, self.order = {}, {}
        n = 0
        for units in self.at:
            for u in units:
                k = n % LANES
                self.bank[u] = k
                self.uses[k] += 1
                self.order[u] = self.uses[k]
                n += 1

    def after(self, times):
        return [b + times * u for b, u in zip(self.before, self.uses)]

    def value(self, it, u):
        k = self.bank[u]
        return it * self.uses[k] + self.before[k] + self.order[u]


def fusion_kernel(nc, x, x_txt, tok_w, pos, nest, seg, txt_w, attn_w, head_w, ln_scale, ln_bias,
                  sh_in, sh_out, sh_out_b, ex_in, ex_out, ex_out_b, group_w, expert_w,
                  group_b, expert_b, pe_table, out):
    ctx = ExitStack()
    text_dram = nc.dram_tensor("text_rows", (B, TXT, D), F32, kind="Internal").ap()
    resid_dram = nc.dram_tensor("resid_rows", (B, P, NT * D), F32, kind="Internal").ap()

    def sb(stack, name, shape, dt=F32):
        return stack.enter_context(nc.sbuf_tensor(name, shape, dt))

    def sem(name):
        return ctx.enter_context(nc.semaphore(name))

    scores = ctx.enter_context(nc.psum_tensor("scores", [P, SB, 512], F32))
    o_ps = ctx.enter_context(nc.psum_tensor("o_ps", [P, 512], F32))
    work = ctx.enter_context(nc.psum_tensor("work", [P, LANES, 512], F32))

    ident = sb(ctx, "ident", [P, P])
    ones = sb(ctx, "ones", [P, DH])
    wqk_hi = sb(ctx, "wqk_hi", [P, 2, H, DH], F32R)
    wqk_lo = sb(ctx, "wqk_lo", [P, 2, H, DH], F32R)
    wv_hi = sb(ctx, "wv_hi", [P, H * DH], F32R)
    wv_lo = sb(ctx, "wv_lo", [P, H * DH], F32R)
    wo = sb(ctx, "wo", [P, PAIRS, D])
    up_hi = sb(ctx, "up_hi", [P, 2, 4, P], F32R)
    up_lo = sb(ctx, "up_lo", [P, 2, 4, P], F32R)
    down_hi = sb(ctx, "down_hi", [P, KC, E * D], F32R)
    down_lo = sb(ctx, "down_lo", [P, KC, E * D], F32R)
    down_sh = sb(ctx, "down_sh", [P, KC, D])
    gate_w = sb(ctx, "gate_w", [P, 2 + E])
    gate_b = sb(ctx, "gate_b", [P, 2 + E])
    ln_cols = sb(ctx, "ln_cols", [P, 2])
    bias_rows = sb(ctx, "bias_rows", [P, 4, D])
    tok_blocks = sb(ctx, "tok_blocks", [P, 4, D])

    loaded = sem("loaded")
    zeroed = sem("zeroed")
    raw_loaded = sem("raw_loaded")
    s_pool = sem("s_pool")
    s_turned = sem("s_turned")
    s_taken = sem("s_taken")
    s_dve = sem("s_dve")
    s_hi = sem("s_hi")
    s_stored = sem("s_stored")
    s_chain = sem("s_chain")

    with ExitStack() as tmp:
        attn_raw = sb(tmp, "attn_raw", [P, 3 * H, DH])
        in_raw = sb(tmp, "in_raw", [P, 2, 4, D])
        out_raw = sb(tmp, "out_raw", [P, 1 + E, HID])
        gates_raw = sb(tmp, "gates_raw", [2 + E, D])
        pos_raw = sb(tmp, "pos_raw", [TXT, D])
        tab_raw = sb(tmp, "tab_raw", [NEST + SEG, D])
        txt_wr = sb(tmp, "txt_wr", [P, 3, D])
        tabs_n = sb(tmp, "tabs_n", [P, NEST + SEG])
        tabs_s = sb(tmp, "tabs_s", [P, NEST + SEG])
        pos_t = sb(tmp, "pos_t", [P, TXT])
        base = sb(tmp, "base", [TXT, D])
        rows24 = sb(tmp, "rows24", [NEST + SEG, D])
        tok_i = sb(tmp, "tok_i", [B, TXT], I32)
        tok = sb(tmp, "tok", [B, TXT])
        opens = sb(tmp, "opens", [B, TXT])
        closes = sb(tmp, "closes", [B, TXT])
        one_b = sb(tmp, "one_b", [B, TXT])
        runs = sb(tmp, "runs", [B, TXT])
        low = sb(tmp, "low", [B, TXT])
        idx = sb(tmp, "idx", [B, 2, TXT])
        idx_t = sb(tmp, "idx_t", [TXT, 2, B])
        iota_e = sb(tmp, "iota_e", [TXT, NEST])
        onehot = sb(tmp, "onehot", [TXT, B, NEST + SEG])
        hot_t = sb(tmp, "hot_t", [NEST + SEG, B, TXT])
        text_h = sb(tmp, "text_h", [TXT, B, D])
        block = tmp.enter_context(nc.Block())

        N_ZEROED = 4

        @block.gpsimd
        def _(pool):
            nc.gpsimd.memset(ident[:], 0.0).then_inc(s_pool, 1)
            pool.wait_ge(s_pool, 1)
            nc.gpsimd.affine_select(out=ident[:], in_=ident[:], compare_op=ALU.not_equal, fill=1.0,
                                    base=0, pattern=[[-1, P]], channel_multiplier=1).then_inc(s_pool, 1)
            nc.gpsimd.iota(iota_e[:], pattern=[[1, NEST]], base=0, channel_multiplier=0,
                           allow_small_or_imprecise_dtypes=True).then_inc(s_pool, 1)

        @block.sync
        def _(sp):
            sp.dma_start(tok_i[:], x_txt).then_inc(loaded, 16)
            sp.dma_start(pos_raw[:], pos[0:TXT, :]).then_inc(raw_loaded, 16)
            sp.dma_start(tab_raw[0:NEST, :], nest).then_inc(raw_loaded, 16)
            sp.dma_start(tab_raw[NEST:NEST + SEG, :], seg).then_inc(raw_loaded, 16)
            sp.dma_start(txt_wr[:], txt_w.rearrange("(a p) n -> p a n", p=P)).then_inc(raw_loaded, 16)
            sp.dma_start(gates_raw[0:2, :], group_w).then_inc(raw_loaded, 16)
            sp.dma_start(gates_raw[2:2 + E, :], expert_w).then_inc(raw_loaded, 16)
            sp.dma_start(in_raw[:, 0], sh_in.rearrange("(a p) n -> p a n", p=P)).then_inc(raw_loaded, 16)
            sp.dma_start(in_raw[:, 1], ex_in.rearrange("(a p) n -> p a n", p=P)).then_inc(raw_loaded, 16)
            sp.dma_start(out_raw[:, 0], sh_out).then_inc(raw_loaded, 16)
            sp.dma_start(out_raw[:, 1:], ex_out.rearrange("e p n -> p e n")).then_inc(raw_loaded, 16)
            sp.dma_start(attn_raw[:], attn_w.rearrange("a p n -> p a n")).then_inc(raw_loaded, 16)
            sp.dma_start(wo[:], head_w.rearrange("(a p) n -> p a n", p=P)).then_inc(raw_loaded, 16)
            sp.dma_start(ln_cols[:, 0:1], ln_scale.rearrange("(p a) -> p a", a=1)).then_inc(raw_loaded, 16)
            sp.dma_start(ln_cols[:, 1:2], ln_bias.rearrange("(p a) -> p a", a=1)).then_inc(raw_loaded, 16)
            sp.dma_start(gate_b[:, 0:2], group_b.rearrange("(a n) -> a n", a=1).broadcast_to((P, 2))).then_inc(raw_loaded, 16)
            sp.dma_start(gate_b[:, 2:2 + E], expert_b.rearrange("(a n) -> a n", a=1).broadcast_to((P, E))).then_inc(raw_loaded, 16)
            sp.wait_ge(zeroed, N_ZEROED)
            for q in range(4):
                sp.dma_start(bias_rows[32 * q:32 * q + E, q, :], ex_out_b).then_inc(raw_loaded, 16)
                sp.dma_start(bias_rows[32 * q + E:32 * q + E + 1, q, :],
                             sh_out_b.rearrange("(a n) -> a n", a=1)).then_inc(raw_loaded, 16)
                sp.dma_start(tok_blocks[32 * q:32 * q + F, q, :], tok_w).then_inc(raw_loaded, 16)
            sp.wait_ge(s_taken, 11)
            sp.dma_start(text_dram.rearrange("b t d -> t b d"), text_h[:]).then_inc(s_stored, 16)
            sp.wait_ge(s_stored, 16)
            sp.wait_ge(raw_loaded, 16 * 28)

        in_turns = [(in_raw[:, w, a, :], P) for w in range(2) for a in range(4)]
        out_turns = [(out_raw[:, e, k * P:(k + 1) * P], P) for e in range(1 + E) for k in range(KC)]
        turns = in_turns + out_turns
        groups = [turns[n:n + 4] for n in range(0, len(turns), 4)]
        NG = len(groups)

        @block.tensor
        def _(pe):
            pe.wait_ge(raw_loaded, 16 * 28)
            pe.wait_ge(s_pool, 2)
            nc.tensor.transpose(work[:, 0, 0:2 + E], gates_raw[:], ident[0:2 + E, 0:2 + E])
            nc.tensor.transpose(work[:, 0, 16:16 + TXT], pos_raw[:], ident[0:TXT, 0:TXT])
            nc.tensor.transpose(work[:, 0, 128:128 + NEST + SEG], tab_raw[:],
                                ident[0:NEST + SEG, 0:NEST + SEG]).then_inc(s_turned, 1)
            pe.wait_ge(s_dve, 1)
            nc.tensor.transpose(work[0:TXT, 1, 0:B], idx[:, 0, :], ident[0:B, 0:B])
            nc.tensor.transpose(work[0:TXT, 1, B:2 * B], idx[:, 1, :], ident[0:B, 0:B]).then_inc(s_turned, 1)
            pe.wait_ge(s_taken, 1)
            nc.tensor.matmul(work[0:TXT, 2, 0:D], pos_t[:], txt_wr[:, 0, :], start=True, stop=True)
            nc.tensor.matmul(work[0:NEST + SEG, 2, D:2 * D], tabs_n[:], txt_wr[:, 1, :], start=True, stop=False)
            nc.tensor.matmul(work[0:NEST + SEG, 2, D:2 * D], tabs_s[:], txt_wr[:, 2, :],
                             start=False, stop=True).then_inc(s_turned, 1)
            pe.wait_ge(s_taken, 3)
            for g in range(4):
                for i in range(4):
                    last = nc.tensor.transpose(work[0:NEST + SEG, g, i * TXT:(i + 1) * TXT],
                                               onehot[:, 4 * g + i, :], ident[0:TXT, 0:TXT])
                last.then_inc(s_turned, 1)
            for g in range(4):
                pe.wait_ge(s_taken, 4 + g)
                for i in range(4):
                    last = nc.tensor.matmul(work[0:TXT, g, i * D:(i + 1) * D],
                                            hot_t[:, 4 * g + i, :], rows24[:], start=True, stop=True)
                last.then_inc(s_turned, 1)
            for g, group in enumerate(groups):
                pe.wait_ge(s_taken, 8 + g)
                for i, (src, _) in enumerate(group):
                    last = nc.tensor.transpose(work[:, g % LANES, i * P:(i + 1) * P], src, ident[:])
                last.then_inc(s_turned, 1)

        @block.scalar
        def _(act):
            act.wait_ge(raw_loaded, 16 * 28)
            v = attn_raw[:].rearrange("p (h w) n -> p w h n", w=3)
            nc.scalar.copy(wqk_hi[:, 0], v[:, 0])
            nc.scalar.copy(wqk_hi[:, 1], v[:, 1])
            nc.scalar.copy(wv_hi[:].rearrange("p (h n) -> p h n", h=H), v[:, 2]).then_inc(s_hi, 1)
            for g, group in enumerate(groups):
                act.wait_ge(s_turned, 12 + g)
                w = work[:, g % LANES, :]
                if g < 2:
                    nc.scalar.copy(up_hi[:, g].rearrange("p a n -> p (a n)"), w).then_inc(s_hi, 1)
                    continue
                for i in range(len(group)):
                    m = 4 * (g - 2) + i
                    e, k = m // KC, m % KC
                    dst = down_sh[:, k, :] if e == 0 else down_hi[:, k, (e - 1) * D:e * D]
                    ins = nc.scalar.copy(dst, w[:, i * P:(i + 1) * P])
                ins.then_inc(s_hi, 1)

        @block.vector
        def _(dve):
            nc.vector.memset(bias_rows[:], 0.0).then_inc(zeroed, 1)
            nc.vector.memset(tok_blocks[:], 0.0).then_inc(zeroed, 1)
            nc.vector.memset(ones[:], 1.0).then_inc(zeroed, 1)
            nc.vector.memset(one_b[:], 1.0).then_inc(zeroed, 1)
            done = [0]
            chain = s_chain

            def then(ins):
                done[0] += 1
                ins.then_inc(chain, 1)
                dve.wait_ge(chain, done[0])

            dve.wait_ge(loaded, 16)
            dve.wait_ge(zeroed, N_ZEROED)
            then(nc.vector.tensor_copy(tok[:], tok_i[:]))
            for mark, codes in ((opens, (40.0, 123.0, 91.0)), (closes, (41.0, 125.0, 93.0))):
                then(nc.vector.tensor_scalar(mark[:], tok[:], codes[0], None, ALU.is_equal))
                for code in codes[1:]:
                    then(nc.vector.scalar_tensor_tensor(out=mark[:], in0=tok[:], scalar=code, in1=mark[:],
                                                        op0=ALU.is_equal, op1=ALU.add))
            then(nc.vector.tensor_tensor(opens[:], opens[:], closes[:], ALU.subtract))
            then(nc.vector.tensor_tensor_scan(runs[:], one_b[:], opens[:], 0.0, ALU.mult, ALU.add))
            then(nc.vector.tensor_tensor_scan(low[:], runs[:], runs[:], 0.0, ALU.min, ALU.min))
            then(nc.vector.tensor_tensor(opens[:], runs[:], low[:], ALU.subtract))
            then(nc.vector.tensor_scalar(idx[:, 0, :], opens[:], 0.0, float(NEST - 1), ALU.max, ALU.min))
            then(nc.vector.tensor_scalar(closes[:], tok[:], 39990.0, None, ALU.is_gt))
            then(nc.vector.tensor_tensor_scan(runs[:], one_b[:], closes[:], 0.0, ALU.mult, ALU.add))
            then(nc.vector.tensor_copy(low[:], runs[:]))
            for m in range(8, TXT + 1, 8):
                then(nc.vector.tensor_scalar(closes[:], runs[:], float(m), -8.0, ALU.is_ge, ALU.mult))
                then(nc.vector.tensor_tensor(low[:], low[:], closes[:], ALU.add))
            nc.vector.tensor_copy(idx[:, 1, :], low[:]).then_inc(s_dve, 1)
            dve.wait_ge(s_turned, 1)
            nc.vector.tensor_copy(gate_w[:], work[:, 0, 0:2 + E])
            nc.vector.tensor_copy(pos_t[:], work[:, 0, 16:16 + TXT])
            nc.vector.memset(tabs_n[:, NEST:], 0.0)
            nc.vector.memset(tabs_s[:, 0:NEST], 0.0)
            nc.vector.tensor_copy(tabs_n[:, 0:NEST], work[:, 0, 128:128 + NEST])
            nc.vector.tensor_copy(tabs_s[:, NEST:], work[:, 0, 128 + NEST:128 + NEST + SEG]).then_inc(s_taken, 1)
            dve.wait_ge(s_turned, 2)
            then(nc.vector.tensor_copy(idx_t[:].rearrange("p a b -> p (a b)"), work[0:TXT, 1, 0:2 * B]))
            dve.wait_ge(s_pool, 3)
            for w, (a, n) in enumerate(((0, NEST), (NEST, SEG))):
                last = nc.vector.tensor_tensor(onehot[:, :, a:a + n],
                                               idx_t[:, w, :].unsqueeze(2).broadcast_to((TXT, B, n)),
                                               iota_e[:, 0:n].unsqueeze(1).broadcast_to((TXT, B, n)), ALU.is_equal)
            last.then_inc(s_taken, 1)
            dve.wait_ge(s_turned, 3)
            then(nc.vector.tensor_copy(base[:], work[0:TXT, 2, 0:D]))
            nc.vector.tensor_copy(rows24[:], work[0:NEST + SEG, 2, D:2 * D]).then_inc(s_taken, 1)
            for g in range(4):
                dve.wait_ge(s_turned, 4 + g)
                nc.vector.tensor_copy(hot_t[:, 4 * g:4 * g + 4, :].rearrange("p a b -> p (a b)"),
                                      work[0:NEST + SEG, g, 0:4 * TXT]).then_inc(s_taken, 1)
            for g in range(4):
                dve.wait_ge(s_turned, 8 + g)
                nc.vector.tensor_tensor(text_h[:, 4 * g:4 * g + 4, :],
                                        work[0:TXT, g, :].rearrange("p (a b) -> p a b", a=4),
                                        base[:].unsqueeze(1).broadcast_to((TXT, 4, D)), ALU.add).then_inc(s_taken, 1)
            for g, group in enumerate(groups):
                dve.wait_ge(s_hi, 2 + g)
                w = work[:, g % LANES, :]
                if g < 2:
                    nc.vector.tensor_tensor(up_lo[:, g].rearrange("p a n -> p (a n)"), w,
                                            up_hi[:, g].rearrange("p a n -> p (a n)"), ALU.subtract).then_inc(s_taken, 1)
                    continue
                for i in range(len(group)):
                    m = 4 * (g - 2) + i
                    e, k = m // KC, m % KC
                    if e > 0:
                        cols = slice((e - 1) * D, e * D)
                        ins = nc.vector.tensor_tensor(down_lo[:, k, cols], w[:, i * P:(i + 1) * P],
                                                      down_hi[:, k, cols], ALU.subtract)
                ins.then_inc(s_taken, 1)
            v = attn_raw[:].rearrange("p (h w) n -> p w h n", w=3)
            nc.vector.tensor_tensor(wqk_lo[:, 0], v[:, 0], wqk_hi[:, 0], ALU.subtract)
            nc.vector.tensor_tensor(wqk_lo[:, 1], v[:, 1], wqk_hi[:, 1], ALU.subtract)
            nc.vector.tensor_tensor(wv_lo[:].rearrange("p (h n) -> p h n", h=H), v[:, 2],
                                    wv_hi[:].rearrange("p (h n) -> p h n", h=H), ALU.subtract)

    yt_hi = sb(ctx, "yt_hi", [P, TW], F32R)
    yt_lo = sb(ctx, "yt_lo", [P, TW], F32R)
    q_a = [[sb(ctx, f"q_a{r}{i}", [P, TP], F32R) for i in range(2)] for r in range(2)]
    k_a = [[sb(ctx, f"k_a{r}{i}", [P, TP], F32R) for i in range(2)] for r in range(2)]
    q_b = [[sb(ctx, f"q_b{r}{i}", [P, TP], F32R) for i in range(2)] for r in range(2)]
    k_b = [[sb(ctx, f"k_b{r}{i}", [P, TP], F32R) for i in range(2)] for r in range(2)]
    values = sb(ctx, "values", [P, NT, H * DH])
    probs = sb(ctx, "probs", [P, NP, 2, CHUNK])
    sums = sb(ctx, "sums", [P, 2, 2, CHUNK])
    heads_t = sb(ctx, "heads_t", [P, PAIRS, TW])
    part_max = sb(ctx, "part_max", [P, 2 * NT, NC])
    neg_max = sb(ctx, "neg_max", [P, 2 * NT])
    max_rows = sb(ctx, "max_rows", [2 * NT, P], F32R)
    h_in = sb(ctx, "h_in", [P, NT, D])
    h_out = sb(ctx, "h_out", [P, NT, D])
    normed = sb(ctx, "normed", [P, NT * D])
    x_t = normed[:, 0:2 * P]
    counts = sb(ctx, "counts", [P, 12, 32])
    counts_t = sb(ctx, "counts_t", [P, 3 * P])
    flat_hi = sb(ctx, "flat_hi", [P, GW], F32R)
    flat_lo = sb(ctx, "flat_lo", [P, GW], F32R)
    hid = sb(ctx, "hid", [P, 2, KC, GW])
    hid_hi = sb(ctx, "hid_hi", [P, KC, GW], F32R)
    hid_lo = sb(ctx, "hid_lo", [P, KC, GW], F32R)
    stats = sb(ctx, "stats", [P, NT, 6])
    mean2 = sb(ctx, "mean2", [P, NT])
    neg_mean = [sb(ctx, f"neg_mean{n}", [P, NT]) for n in range(2)]
    mdiff = sb(ctx, "mdiff", [P, NT])
    msq = sb(ctx, "msq", [P, NT])
    var = [sb(ctx, f"var_{n}", [P, NT]) for n in range(2)]
    minus_half = sb(ctx, "minus_half", [P, NT])
    rstd = [sb(ctx, f"rstd_{n}", [P, NT]) for n in range(2)]
    shift = [sb(ctx, f"shift_{n}", [P, NT]) for n in range(2)]
    logits = sb(ctx, "logits", [P, NT, 2 + E])
    g_on = sb(ctx, "g_on", [P, 2, NT])
    e_sel = sb(ctx, "e_sel", [P, NT, EG])
    e_tmp = sb(ctx, "e_tmp", [P, NT, EG])
    e_exp = sb(ctx, "e_exp", [P, NT, EG])
    e_max = sb(ctx, "e_max", [P, NT])
    rank = sb(ctx, "rank", [P, NT, EG])
    beats = sb(ctx, "beats", [P, 3, NT, 3])
    four = sb(ctx, "four", [P, EG])
    den = sb(ctx, "den", [P, 2, NT])
    comb = sb(ctx, "comb", [P, NT, E])

    filled = [sem(f"work_filled{k}") for k in range(LANES)]
    drained = [sem(f"work_drained{k}") for k in range(LANES)]
    x_loaded = sem("x_loaded")
    seeded = sem("seeded")
    resid_stored = sem("resid_stored")
    resid_loaded = sem("resid_loaded")
    out_stored = sem("out_stored")
    max_loaded = sem("max_loaded")
    scores_ready = sem("scores_ready")
    probs_ready = sem("probs_ready")
    probs_used = sem("probs_used")
    sums_done = sem("sums_done")
    heads_out = sem("heads_out")
    heads_scaled = sem("heads_scaled")
    qk_hi = sem("qk_hi")
    max_ready = sem("max_ready")
    yt_hi_ready = sem("yt_hi_ready")
    var_ready = [sem(f"var_ready{n}") for n in range(2)]
    rstd_ready = [sem(f"rstd_ready{n}") for n in range(2)]
    shift_ready = [sem(f"shift_ready{n}") for n in range(2)]
    norm_ready = [sem(f"norm_ready{n}") for n in range(2)]
    flat_split = sem("flat_split")
    sel_ready = sem("sel_ready")
    sel_exp = sem("sel_exp")
    counted = sem("counted")
    tanh_ready = sem("tanh_ready")
    hid_hi_ready = sem("hid_hi_ready")
    hid_split = sem("hid_split")
    sp_passed = sem("sp_passed")
    cleared = sem("cleared")
    prepared = sem("prepared")
    PREPARED = 2

    last_max = [maxima(p)[0][-1] for p in range(PAIRS)]
    max_needs = {}
    for p in range(PAIRS):
        max_needs.update(maxima(p)[1])

    pro = Segment(False, False, True, [0] * LANES)
    first = Segment(True, False, True, pro.after(1))
    loop = Segment(True, True, True, first.after(1))
    last = Segment(True, True, False, loop.after(B - 2))
    epi = Segment(False, True, False, last.after(1))

    def wait(eng, s, v):
        if not isinstance(v, int) or v > 0:
            eng.wait_ge(s, v)

    def wait_filled(eng, seg, it, u):
        wait(eng, filled[seg.bank[u]], seg.value(it, u))

    def wait_drained(eng, seg, it, *units):
        for k in range(LANES):
            of_bank = [u for u in units if seg.bank[u] == k]
            if of_bank:
                wait(eng, drained[k], seg.value(it, max(of_bank, key=seg.order.get)))

    def wait_bank(eng, seg, it, u, *needed):
        wait(eng, drained[seg.bank[u]], seg.value(it, u) - 1)
        wait_drained(eng, seg, it, *[n for n in needed if seg.bank[n] != seg.bank[u]])

    def run(eng, step):
        def iteration(seg, it, b):
            for s in range(ALL):
                step(seg, it, b, s)
        iteration(pro, 0, -1)
        iteration(first, 0, 0)
        with eng.Fori(1, B - 1) as b:
            iteration(loop, b - 1, b)
        iteration(last, 0, B - 1)
        iteration(epi, 0, B)

    def cut(s):
        return s // STEPS, s % STEPS // NT, s % NT

    def summed(s):
        return (NT - 1) * (s // NT) + max(s % NT, 1)

    block = ctx.enter_context(nc.Block())

    @block.tensor
    def _(pe):
        def needs(u):
            if u in (("v", 0, 0), ("qk", 0, "k", 0)):
                return [("turn1", g) for g in range(3)]
            if u[0] == "max":
                return max_needs.get(u, [])
            if u[0] == "gate":
                return [("turn2", g) for g in range(3)]
            if u[0] == "shared":
                return [("up", u[1] // 3, 0, k, 1) for k in range(KC)] + [("count",)]
            if u[0] == "embed":
                return [("turnx",)]
            return []

        def unit(seg, it, b, u):
            k, kind = seg.bank[u], u[0]
            w = work[:, k, :]
            wait_bank(pe, seg, it, u, *needs(u))
            if kind == "v":
                _, half, j = u
                cols = slice(half * HALF, (half + 1) * HALF)
                for n, (y, wv) in enumerate(((yt_hi, wv_hi), (yt_lo, wv_hi), (yt_hi, wv_lo))):
                    mm = nc.tensor.matmul(w[:, 0:HALF], y[:, j * P:(j + 1) * P], wv[:, cols],
                                          start=(n == 0), stop=(n == 2))
            elif kind == "qk":
                _, p, what, c = u
                m = "qk".index(what)
                c0, cw = CHUNKS[c]
                for n, (wt, y) in enumerate(((wqk_hi, yt_hi), (wqk_hi, yt_lo), (wqk_lo, yt_hi))):
                    mm = nc.tensor.matmul(w[:, 0:cw], wt[:, m, 2 * p:2 * p + 2, :].rearrange("p a n -> p (a n)"),
                                          y[:, c0:c0 + cw], start=(n == 0), stop=(n == 2))
            elif kind == "max":
                _, p, i, j, c = u
                c0, cw = CHUNKS[c]
                n = queries(j)
                mm = nc.tensor.matmul(w[0:n, 0:cw], q_a[p % 2][i][:, j * P:j * P + n],
                                      k_a[p % 2][i][:, c0:c0 + cw], start=True, stop=True)
            elif kind == "maxrow":
                pe.wait_ge(max_ready, PAIRS * b + (u[1] - 1) % PAIRS + 2)
                mm = nc.tensor.transpose(w[0:2 * NT, 0:P], neg_max[:], ident[:])
            elif kind == "sum":
                q = u[1]
                bb = b - 1 if q == PAIRS * NC - 1 else b
                pe.wait_ge(sums_done, (NT - 1) * (PAIRS * NC * bb + q + 1))
                cw = CHUNKS[q % NC][1]
                for i in range(2):
                    mm = nc.tensor.matmul(w[64 * i:64 * i + 64, 0:cw], ones[:], sums[:, q % 2, i, 0:cw],
                                          start=True, stop=True)
            elif kind == "proj":
                j = u[1]
                if j == 0:
                    pe.wait_ge(heads_scaled, PAIRS * NC * b - 1)
                if (j + 1) * P > CHUNKS[-1][0] and j * P <= CHUNKS[-1][0]:
                    pe.wait_ge(heads_scaled, PAIRS * NC * b)
                for p in range(PAIRS):
                    mm = nc.tensor.matmul(w[:, 0:D], heads_t[:, p, j * P:(j + 1) * P], wo[:, p, :],
                                          start=(p == 0), stop=(p == PAIRS - 1))
            elif kind in ("turn1", "turn2"):
                g, n = u[1], int(kind == "turn2")
                item = b - 1 if n else b + 1
                pe.wait_ge(norm_ready[n], NT * item + 3 * g + 3)
                for j in range(3):
                    mm = nc.tensor.transpose(w[:, j * P:(j + 1) * P],
                                             normed[:, (3 * g + j) * P:(3 * g + j + 1) * P], ident[:])
            elif kind == "gate":
                for j in range(NT):
                    mm = nc.tensor.matmul(w[:, j * (2 + E):(j + 1) * (2 + E)], normed[:, j * P:(j + 1) * P],
                                          gate_w[:], start=True, stop=True)
            elif kind == "count":
                pe.wait_ge(counted, b)
                for g in range(3):
                    mm = nc.tensor.transpose(w[:, g * P:(g + 1) * P],
                                             counts[:, 4 * g:4 * g + 4, :].rearrange("p a n -> p (a n)"), ident[:])
            elif kind == "up":
                _, c, path, k2, half = u
                pe.wait_ge(flat_split, 3 * (b - 1) + c + 1)
                m = 2 * half + k2
                for n, (wt, y) in enumerate(((up_hi, flat_hi), (up_hi, flat_lo), (up_lo, flat_hi))):
                    mm = nc.tensor.matmul(w[:, 0:GW], wt[:, path, m, :], y[:],
                                          start=(n == 0), stop=(n == 2))
            elif kind == "shared":
                t = u[1]
                for k2 in range(KC):
                    nc.tensor.matmul(w[:, 0:D], hid[:, 0, k2, t % 3 * P:(t % 3 + 1) * P], down_sh[:, k2, :],
                                     start=(k2 == 0), stop=False)
                mm = nc.tensor.matmul(w[:, 0:D], counts_t[:, t // 4 * P:(t // 4 + 1) * P], bias_rows[:, t % 4, :],
                                      start=False, stop=True)
            elif kind == "expert":
                _, t, g = u
                pe.wait_ge(hid_split, 3 * KC * (b - 1) + KC * (t // 3 + 1))
                cols = slice(t % 3 * P, (t % 3 + 1) * P)
                ops = [(k2, h, wt) for k2 in range(KC)
                       for h, wt in ((hid_hi, down_hi), (hid_lo, down_hi), (hid_hi, down_lo))]
                for n, (k2, h, wt) in enumerate(ops):
                    mm = nc.tensor.matmul(w, h[:, k2, cols], wt[:, k2, g * EG * D:(g + 1) * EG * D],
                                          start=(n == 0), stop=(n == len(ops) - 1))
            elif kind == "turnx":
                pe.wait_ge(x_loaded, 16 * (b + 2))
                if seg.post:
                    pe.wait_ge(flat_split, 3 * b)
                for g in range(2):
                    mm = nc.tensor.transpose(w[:, g * P:(g + 1) * P],
                                             counts[:, 4 * g:4 * g + 4, :].rearrange("p a n -> p (a n)"), ident[:])
            elif kind == "embed":
                g = u[1]
                mm = nc.tensor.matmul(w, x_t[:, g * P:(g + 1) * P], tok_blocks[:].rearrange("p a n -> p (a n)"),
                                      start=True, stop=True)
            mm.then_inc(filled[k], 1)

        def score(seg, b, s):
            p, c, t = cut(s)
            if s % STEPS == 0:
                pe.wait_ge(max_loaded, 64 * (PAIRS * b + p + 1))
            c0, cw = CHUNKS[c]
            n = rows(t)
            for i in range(2):
                h = 2 * s + i
                wait(pe, probs_ready, 2 * ALL * b + h - SB + 1)
                o = scores[0:n, h % SB, 0:cw]
                nc.tensor.matmul(o, k_a[p % 2][i][:, t * P:t * P + n], q_a[p % 2][i][:, c0:c0 + cw],
                                 start=True, stop=False)
                nc.tensor.matmul(o, k_b[p % 2][i][:, t * P:t * P + n], q_b[p % 2][i][:, c0:c0 + cw],
                                 start=False, stop=True).then_inc(scores_ready, 1)

        def weigh(seg, it, b, s):
            p, c, t = cut(s)
            pe.wait_ge(probs_ready, 2 * (ALL * b + s + 1))
            if s == 0:
                for k in range(LANES):
                    wait(pe, drained[k], it * seg.uses[k] + seg.before[k])
            if s == ALL // 2:
                wait_drained(pe, seg, it, *[("v", 1, j) for j in range(NT)])
            if t == 0:
                wait(pe, heads_out, PAIRS * NC * b + s // NT)
            cw, n = CHUNKS[c][1], rows(t)
            for i in range(2):
                h = 2 * p + i
                mm = nc.tensor.matmul(o_ps[64 * i:64 * i + 64, 0:cw], values[0:n, t, h * DH:(h + 1) * DH],
                                      probs[0:n, s % NP, i, 0:cw], start=(t == 0), stop=(t == NT - 1))
            mm.then_inc(probs_used, 1)

        def step(seg, it, b, s):
            units = seg.at[s]
            if seg.attn:
                score(seg, b, s)
            if s == 0 and seg.ends:
                weigh(seg, it, b - 1, ALL - 1)
            if seg.attn and s > 0:
                early = len(units) // 2 if s % NT else 0
                for u in units[:early]:
                    unit(seg, it, b, u)
                units = units[early:]
                weigh(seg, it, b, s - 1)
            for u in units:
                unit(seg, it, b, u)

        pe.wait_ge(prepared, PREPARED)
        run(pe, step)

    @block.scalar
    def _(act):
        def unit(seg, it, b, u):
            k, kind = seg.bank[u], u[0]
            w = work[:, k, :]
            if kind not in ("v", "qk", "sum", "turn1", "turn2", "count", "up", "turnx") or (kind == "up" and u[4]):
                return
            wait_filled(act, seg, it, u)
            if kind == "v":
                _, half, j = u
                wait(act, probs_used, ALL * b if half else ALL * b + ALL // 2)
                nc.scalar.copy(values[:, j, half * HALF:(half + 1) * HALF], w[:, 0:HALF]).then_inc(drained[k], 1)
            elif kind == "qk":
                _, p, what, c = u
                c0, cw = CHUNKS[c]
                for i in range(2):
                    src = w[64 * i:64 * i + 64, 0:cw]
                    a, z = (k_a, k_a) if what == "k" else (q_a, q_b)
                    nc.scalar.copy(a[p % 2][i][0:64, c0:c0 + cw], src)
                    o = 64 if what == "k" else 0
                    nc.scalar.copy(z[p % 2][i][o:o + 64, c0:c0 + cw], src).then_inc(qk_hi, 1)
            elif kind == "sum":
                q = u[1]
                cw = CHUNKS[q % NC][1]
                nc.scalar.copy(sums[:, q % 2, 0, 0:cw], w[:, 0:cw]).then_inc(drained[k], 1)
            elif kind == "turn1":
                g = u[1]
                nc.scalar.copy(yt_hi[:, g * GW:(g + 1) * GW], w[:, 0:GW]).then_inc(yt_hi_ready, 1)
            elif kind == "turn2":
                g = u[1]
                nc.scalar.activation(normed[:, g * GW:(g + 1) * GW], w[:, 0:GW], ACT.Identity,
                                     bias=ln_cols[:, 1:2], scale=ln_cols[:, 0:1]).then_inc(drained[k], 1)
            elif kind == "count":
                nc.scalar.copy(counts_t[:], w[:, 0:3 * P]).then_inc(drained[k], 1)
            elif kind == "turnx":
                nc.scalar.copy(x_t, w[:, 0:2 * P]).then_inc(drained[k], 1)
            elif kind == "up":
                _, c, path, k2, half = u
                nc.scalar.activation(hid[:, path, k2, :], w[:, 0:GW], ACT.Tanh, scale=0.5).then_inc(tanh_ready, 1)

        def normalise(n, item, src, g):
            act.wait_ge(shift_ready[n], item + 1)
            for j in range(3 * g, 3 * g + 3):
                nc.scalar.activation(normed[:, j * D:(j + 1) * D], src[:, j, :], ACT.Identity,
                                     bias=shift[n][:, j:j + 1], scale=rstd[n][:, j:j + 1]).then_inc(norm_ready[n], 1)

        def heads(seg, it, b, q):
            act.wait_ge(probs_used, ALL * b + NT * (q + 1))
            if q < NC and seg.post:
                wait_filled(act, seg, it, ("proj", 3 * q + 2))
            c0, cw = CHUNKS[q % NC]
            nc.scalar.copy(heads_t[:, q // NC, c0:c0 + cw], o_ps[:, 0:cw]).then_inc(heads_out, 1)

        def step(seg, it, b, s):
            if seg.attn:
                p, c, t = cut(s)
                wait(act, probs_used, ALL * b + s - NP + 1)
                if not isinstance(b, int) or b > 0 or s >= NP:
                    wait(act, sums_done, (NT - 1) * PAIRS * NC * b + summed(s - NP))
                cw, n = CHUNKS[c][1], rows(t)
                for i in range(2):
                    h = 2 * s + i
                    act.wait_ge(scores_ready, 2 * ALL * b + h + 1)
                    nc.scalar.activation(probs[0:n, s % NP, i, 0:cw], scores[0:n, h % SB, 0:cw], ACT.Exp,
                                         scale=DH ** -0.5).then_inc(probs_ready, 1)
                if t == 0 and s > 0:
                    heads(seg, it, b, s // NT - 1)
            if s == 0 and seg.ends:
                heads(seg, it, b - 1, PAIRS * NC - 1)
            if seg.post and s == GATE + 2:
                act.wait_ge(sel_ready, b)
                nc.scalar.activation(e_exp[:], e_sel[:], ACT.Exp).then_inc(sel_exp, 1)
            for u in seg.at[s]:
                unit(seg, it, b, u)
            if seg.post and TURN - 2 <= s <= TURN:
                normalise(1, b - 1, h_out, s - TURN + 2)
            if seg.prep and EMBED + 8 <= s <= EMBED + 10:
                normalise(0, b + 1, h_in, s - EMBED - 8)
            for u in seg.at[s - 1] if s > 0 else []:
                if load(u) == LOAD["upx"]:
                    wait_drained(act, seg, it, u)
                    nc.scalar.copy(hid_hi[:, u[3], :], hid[:, 1, u[3], :]).then_inc(hid_hi_ready, 1)

        act.wait_ge(prepared, PREPARED)
        run(act, step)

    @block.vector
    def _(dve):
        done = [0]
        inverted = {}

        def then(ins):
            done[0] += 1
            ins.then_inc(s_chain, 1)
            dve.wait_ge(s_chain, done[0])

        def unit(seg, it, b, u):
            k, kind = seg.bank[u], u[0]
            w = work[:, k, :]
            if kind in ("v", "sum", "turn2", "count", "turnx"):
                return
            wait_filled(dve, seg, it, u)
            if kind == "qk":
                _, p, what, c = u
                c0, cw = CHUNKS[c]
                n = 12 * (PAIRS * b + (p - 1) % PAIRS + 1) + 4 * c + 2 * "kq".index(what)
                for i in range(2):
                    dve.wait_ge(qk_hi, n + i + 1)
                    src = w[64 * i:64 * i + 64, 0:cw]
                    if what == "k":
                        ins = nc.vector.tensor_tensor(k_b[p % 2][i][0:64, c0:c0 + cw], src,
                                                      k_a[p % 2][i][0:64, c0:c0 + cw], ALU.subtract)
                    else:
                        ins = nc.vector.tensor_tensor(q_a[p % 2][i][64:128, c0:c0 + cw], src,
                                                      q_b[p % 2][i][0:64, c0:c0 + cw], ALU.subtract)
                ins.then_inc(drained[k], 1)
            elif kind == "max":
                _, p, i, j, c = u
                n = queries(j)
                keys = min(CHUNKS[c][1], T - CHUNKS[c][0])
                nc.vector.tensor_reduce(part_max[0:n, i * NT + j, c:c + 1], w[0:n, 0:keys], AX.X,
                                        ALU.max).then_inc(drained[k], 1)
                if u == last_max[p]:
                    wait_drained(dve, seg, it, u)
                    nc.vector.tensor_reduce(neg_max[:], part_max[:], AX.X, ALU.max, negate=True).then_inc(max_ready, 1)
            elif kind == "maxrow":
                wait(dve, max_loaded, 64 * (PAIRS * b + (u[1] - 1) % PAIRS + 1))
                nc.vector.tensor_copy(max_rows[:], w[0:2 * NT, 0:P]).then_inc(drained[k], 1)
            elif kind == "proj":
                j = u[1]
                dve.wait_ge(resid_loaded, 16 * b)
                nc.vector.tensor_tensor(h_out[:, j, :], w[:, 0:D], h_out[:, j, :], ALU.add).then_inc(drained[k], 1)
            elif kind == "turn1":
                g = u[1]
                dve.wait_ge(yt_hi_ready, 3 * (b + 1) + g + 1)
                cols = slice(g * GW, (g + 1) * GW)
                nc.vector.tensor_tensor(yt_lo[:, cols], w[:, 0:GW], yt_hi[:, cols], ALU.subtract).then_inc(drained[k], 1)
            elif kind == "gate":
                nc.vector.tensor_tensor(logits[:], w[:, 0:NT * (2 + E)].rearrange("p (a n) -> p a n", a=NT),
                                        gate_b[:].unsqueeze(1).broadcast_to((P, NT, 2 + E)),
                                        ALU.add).then_inc(drained[k], 1)
                wait_drained(dve, seg, it, u)
                choose_group()
            elif kind == "up":
                _, c, path, k2, half = u
                o = hid[:, path, k2, :]
                if half == 0:
                    dve.wait_ge(tanh_ready, 12 * (b - 1) + 4 * c + 2 * (1 - path) + k2 + 1)
                    nc.vector.scalar_tensor_tensor(out=o, in0=o, scalar=1.0, in1=w[:, 0:GW], op0=ALU.add,
                                                   op1=ALU.mult).then_inc(drained[k], 1)
                else:
                    wait_drained(dve, seg, it, ("up", c, path, k2, 0))
                    nc.vector.scalar_tensor_tensor(out=o, in0=o, scalar=0.5, in1=w[:, 0:GW], op0=ALU.mult,
                                                   op1=ALU.mult).then_inc(drained[k], 1)
                if u[2:] == (0, 1, 1) and c < 2:
                    split_flat(seg, it, c + 1)
            elif kind == "shared":
                t = u[1]
                nc.vector.tensor_tensor(h_out[:, t, :], w[:, 0:D], h_out[:, t, :], ALU.add).then_inc(drained[k], 1)
            elif kind == "expert":
                _, t, g = u
                wait_drained(dve, seg, it, ("expert", t, 0) if g else ("shared", t))
                o = h_out[:, t, :]
                for e in range(EG):
                    ins = nc.vector.scalar_tensor_tensor(
                        out=o, in0=w[:, e * D:(e + 1) * D], scalar=comb[:, t, g * EG + e:g * EG + e + 1],
                        in1=o, op0=ALU.mult, op1=ALU.add)
                    if e < EG - 1:
                        then(ins)
                ins.then_inc(drained[k], 1)
            elif kind == "embed":
                g = u[1]
                wait(dve, seeded, 32 * (b + 2))
                o = h_in[:, 4 * g:4 * g + 4, :].rearrange("p a n -> p (a n)")
                nc.vector.tensor_tensor(o, w, o, ALU.add).then_inc(drained[k], 1)

        def divide(seg, it, b, q, part):
            n = PAIRS * NC * (b - 1 if q == PAIRS * NC - 1 else b) + q
            c0, cw = CHUNKS[q % NC]
            inverse = sums[:, q % 2, 0, :]
            if part == 0:
                wait_drained(dve, seg, it, ("sum", q))
            if part < DIV:
                cols = slice(part * CHUNK // DIV, min((part + 1) * CHUNK // DIV, cw))
                done[0] += 1
                nc.vector.reciprocal(inverse[:, cols], inverse[:, cols]).then_inc(s_chain, 1)
                inverted[q] = done[0]
            else:
                dve.wait_ge(s_chain, inverted[q])
                dve.wait_ge(heads_out, n + 1)
                o = heads_t[:, q // NC, c0:c0 + cw]
                nc.vector.tensor_tensor(o, inverse[:, 0:cw], o, ALU.mult).then_inc(heads_scaled, 1)

        def split_flat(seg, it, c):
            wait_drained(dve, seg, it, ("turn2", c))
            src = normed[:, c * GW:(c + 1) * GW]
            then(nc.vector.tensor_copy(flat_hi[:], src))
            nc.vector.tensor_tensor(flat_lo[:], src, flat_hi[:], ALU.subtract).then_inc(flat_split, 1)

        def statistics(src, tiles):
            for j in tiles:
                ins = nc.vector.bn_stats(stats[:, j, :], src[:, j, :])
            return ins

        def moments(n):
            nc.vector.tensor_tensor(mean2[:], stats[:, :, 1], stats[:, :, 4], ALU.add)
            nc.vector.tensor_tensor(msq[:], stats[:, :, 2], stats[:, :, 5], ALU.add)
            then(nc.vector.tensor_tensor(mdiff[:], stats[:, :, 1], stats[:, :, 4], ALU.subtract))
            nc.vector.tensor_scalar(neg_mean[n][:], mean2[:], -0.5, None, ALU.mult)
            then(nc.vector.scalar_tensor_tensor(out=mdiff[:], in0=mdiff[:], scalar=0.25, in1=mdiff[:],
                                                op0=ALU.mult, op1=ALU.mult))
            ins = nc.vector.scalar_tensor_tensor(out=var[n][:], in0=msq[:], scalar=1.0 / D, in1=mdiff[:],
                                                 op0=ALU.mult, op1=ALU.add)
            then(ins)
            scale, eps = (1.0 + EPS, EPS * EPS) if n else (1.0, EPS)
            nc.vector.tensor_scalar(var[n][:], var[n][:], scale, eps, ALU.mult, ALU.add).then_inc(var_ready[n], 1)

        def choose_group():
            nc.vector.tensor_tensor(g_on[:, 0, :], logits[:, :, 0], logits[:, :, 1], ALU.is_ge)
            then(nc.vector.tensor_tensor(g_on[:, 1, :], logits[:, :, 1], logits[:, :, 0], ALU.is_gt))
            for g, o in ((0, e_tmp), (1, e_sel)):
                ins = nc.vector.tensor_tensor(o[:], logits[:, :, 2 + g * EG:2 + (g + 1) * EG],
                                              g_on[:, g, :].unsqueeze(2).broadcast_to((P, NT, EG)), ALU.mult)
            then(ins)
            then(nc.vector.tensor_tensor(e_sel[:], e_sel[:], e_tmp[:], ALU.add))
            then(nc.vector.tensor_reduce(e_max[:], e_sel[:], AX.X, ALU.max))

        def rank_experts():
            for d in (1, 2, 3):
                nc.vector.tensor_tensor(beats[:, d - 1, :, 0:EG - d], e_sel[:, :, d:], e_sel[:, :, 0:EG - d], ALU.is_gt)
            then(nc.vector.tensor_copy(rank[:], four[:].unsqueeze(1).broadcast_to((P, NT, EG))))
            nc.vector.tensor_tensor(e_sel[:], e_sel[:], e_max[:].unsqueeze(2).broadcast_to((P, NT, EG)),
                                    ALU.subtract).then_inc(sel_ready, 1)
            for d in (1, 2, 3):
                m = beats[:, d - 1, :, 0:EG - d]
                then(nc.vector.tensor_tensor(rank[:, :, 0:EG - d], rank[:, :, 0:EG - d], m, ALU.add))
                then(nc.vector.tensor_tensor(rank[:, :, d:], rank[:, :, d:], m, ALU.subtract))
            then(nc.vector.tensor_scalar(rank[:], rank[:], 1.5, None, ALU.is_lt))

        def weights(b):
            for g in range(2):
                nc.vector.tensor_tensor(counts[:, 0:NT, g * EG:(g + 1) * EG], rank[:],
                                        g_on[:, g, :].unsqueeze(2).broadcast_to((P, NT, EG)), ALU.mult)
            nc.vector.memset(counts[:, 0:NT, E:E + 1], 1.0).then_inc(counted, 1)
            dve.wait_ge(sel_exp, b)
            nc.vector.tensor_tensor(e_tmp[:], e_exp[:], rank[:], ALU.mult)
            then(nc.vector.tensor_reduce(den[:, 0, :], e_exp[:], AX.X, ALU.add))
            then(nc.vector.tensor_reduce(den[:, 1, :], e_tmp[:], AX.X, ALU.add))
            then(nc.vector.scalar_tensor_tensor(out=den[:, 0, :], in0=den[:, 0, :], scalar=1e-8, in1=den[:, 1, :],
                                                op0=ALU.mult, op1=ALU.add))
            then(nc.vector.reciprocal(den[:, 1, :], den[:, 0, :]))
            then(nc.vector.tensor_tensor(e_tmp[:], e_tmp[:], den[:, 1, :].unsqueeze(2).broadcast_to((P, NT, EG)),
                                         ALU.mult))
            for g in range(2):
                ins = nc.vector.tensor_tensor(comb[:, :, g * EG:(g + 1) * EG], e_tmp[:],
                                              g_on[:, g, :].unsqueeze(2).broadcast_to((P, NT, EG)), ALU.mult)
            then(ins)

        def step(seg, it, b, s):
            if s == 0:
                if done[0]:
                    nc.vector.sem_clear(s_chain)
                done[0] = 0
            for u in seg.at[s - 2] if s > 1 else []:
                if load(u) == LOAD["upx"]:
                    _, c, _, k2, _ = u
                    dve.wait_ge(hid_hi_ready, 3 * KC * (b - 1) + KC * c + k2 + 1)
                    nc.vector.tensor_tensor(hid_lo[:, k2, :], hid[:, 1, k2, :], hid_hi[:, k2, :],
                                            ALU.subtract).then_inc(hid_split, 1)
            for u in seg.at[s]:
                unit(seg, it, b, u)
            for part in range(DIV + 1):
                for u in seg.at[s - 1 - part] if s > part else []:
                    if u[0] == "sum":
                        divide(seg, it, b, u[1], part)
            if seg.post:
                for g in range(3):
                    if s == PROJ[3 * g + 2] + 1:
                        wait_drained(dve, seg, it, *[("proj", j) for j in range(3 * g, 3 * g + 3)])
                        then(statistics(h_out, range(3 * g, 3 * g + 3)))
                if s == STATS:
                    moments(1)
                if s == TURN + 3:
                    split_flat(seg, it, 0)
                if s == GATE + 1:
                    rank_experts()
                if s == WEIGHTS:
                    weights(b)
            if seg.prep:
                for g in range(2):
                    if s == EMBED + 2 + g:
                        wait_drained(dve, seg, it, ("embed", g))
                        then(statistics(h_in, range(4 * g, 4 * g + 4 + g)))
                if s == EMBED + 4:
                    moments(0)

        nc.vector.sem_clear(s_chain)
        nc.vector.memset(counts[:], 0.0)
        nc.vector.memset(h_in[:, IMG, :], 0.0).then_inc(cleared, 1)
        for r in range(2):
            for i in range(2):
                then(nc.vector.memset(k_b[r][i][64:128, :].bitcast(F32), 0.0))
                nc.vector.memset(k_b[r][i][64:65, :].bitcast(F32), 1.0)
        nc.vector.memset(heads_t[:, :, TP:], 0.0)
        nc.vector.memset(part_max[:], 0.0)
        nc.vector.memset(minus_half[:], -0.5)
        nc.vector.memset(four[:, 0:1], 0.0)
        nc.vector.memset(four[:, 1:2], 1.0)
        nc.vector.memset(four[:, 2:3], 2.0)
        nc.vector.memset(four[:, 3:4], 3.0).then_inc(prepared, 1)
        dve.wait_ge(prepared, PREPARED)
        run(dve, step)

    @block.gpsimd
    def _(pool):
        def root(n, item):
            pool.wait_ge(var_ready[n], item + 1)
            nc.gpsimd.tensor_tensor(rstd[n][:], var[n][:], minus_half[:], ALU.pow).then_inc(rstd_ready[n], 1)
            pool.wait_ge(rstd_ready[n], item + 1)
            nc.gpsimd.tensor_tensor(shift[n][:], neg_mean[n][:], rstd[n][:], ALU.mult).then_inc(shift_ready[n], 1)

        def step(seg, it, b, s):
            if seg.post and s == STATS:
                root(1, b - 1)
            if seg.prep and s == EMBED + 4:
                root(0, b + 1)
            if not seg.attn:
                return
            p, c, t = cut(s)
            if t == 0:
                return
            q = s // NT
            cw, n = CHUNKS[c][1], rows(t)
            pool.wait_ge(probs_ready, 2 * (ALL * b + s + 1))
            acc = sums[0:n, q % 2, :, 0:cw]
            if t == 1:
                if not isinstance(b, int) or b > 0 or q >= 2:
                    pool.wait_ge(heads_scaled, PAIRS * NC * b + q - 1)
                nc.gpsimd.tensor_tensor(acc, probs[:, (s - 1) % NP, :, 0:cw], probs[:, s % NP, :, 0:cw],
                                        ALU.add).then_inc(sums_done, 1)
            else:
                pool.wait_ge(sums_done, (NT - 1) * (PAIRS * NC * b + q) + t - 1)
                nc.gpsimd.tensor_tensor(acc, acc, probs[0:n, s % NP, :, 0:cw], ALU.add).then_inc(sums_done, 1)

        for r in range(2):
            for i in range(2):
                ins = nc.gpsimd.memset(q_b[r][i][64:128, :].bitcast(F32), 0.0)
        ins.then_inc(prepared, 1)
        pool.wait_ge(prepared, PREPARED)
        run(pool, step)

    @block.sync
    def _(sp):
        def wait_then(sem_wait, *args):
            sem_wait(*args)
            sp.sem_inc(sp_passed, 1)

        x_rows = x.rearrange("b h w f -> b (h w) f").rearrange("b (p j) f -> b p j f", j=IMG)
        out_img = out[:, 0:HW, :].rearrange("b (p j) d -> b p j d", j=IMG)

        def seed(n):
            sp.dma_start(h_in[:, 0:IMG, :], pe_table.rearrange("(p j) d -> p j d", j=IMG)).then_inc(seeded, 16)
            sp.dma_start(h_in[0:TXT, IMG, :], text_dram[n]).then_inc(seeded, 16)

        def step(seg, it, b, s):
            if seg.post and s == 0:
                wait_then(sp.wait_ge, resid_stored, 16 * b)
                sp.dma_start(h_out[:].rearrange("p a n -> p (a n)"), resid_dram[b - 1]).then_inc(resid_loaded, 16)
            if seg.prep and s == 30:
                if seg.post:
                    wait_then(wait_drained, sp, seg, it, ("count",))
                sp.dma_start(counts[:, 0:IMG, 0:F], x_rows[b + 1]).then_inc(x_loaded, 16)
                wait_then(wait, sp, norm_ready[0], NT * (b + 1))
                seed(b + 1)
            if seg.prep and s == EMBED + 3:
                wait_then(wait_drained, sp, seg, it, ("embed", 1))
                sp.dma_start(resid_dram[b + 1], h_in[:].rearrange("p a n -> p (a n)")).then_inc(resid_stored, 16)
                wait_then(sp.wait_ge, resid_stored, 16 * (b + 2))
            for u in seg.at[s]:
                if u[0] == "maxrow":
                    wait_then(wait_drained, sp, seg, it, u)
                    for i in range(2):
                        row = q_b[u[1] % 2][i][64:65, :].bitcast(F32)
                        r = i * NT
                        sp.dma_start(row[:, 0:HW].rearrange("p (a n) -> p a n", a=IMG),
                                     max_rows[r:r + IMG, :].bitcast(F32)).then_inc(max_loaded, 16)
                        sp.dma_start(row[:, HW:TP], max_rows[r + IMG:r + NT, 0:TP - HW].bitcast(F32)).then_inc(max_loaded, 16)
            if seg.post and s == STORE:
                wait_then(wait_drained, sp, seg, it, ("expert", NT - 1, 1))
                sp.dma_start(out_img[b - 1], h_out[:, 0:IMG, :]).then_inc(out_stored, 16)
                sp.dma_start(out[b - 1, HW:T, :], h_out[0:TXT, IMG, :]).then_inc(out_stored, 16)
                wait_then(sp.wait_ge, out_stored, 32 * b)

        wait_then(sp.wait_ge, cleared, 1)
        run(sp, step)

    ctx.close()


_INS = ['x', 'x_txt', 'L0_tok_W', 'L0_txt_pos_table', 'L0_txt_nest_table', 'L0_txt_seg_table', 'L0_txt_W',
        'L0_attn_kernel', 'L0_attn_head_kernel', 'L0_ffn_ln_scale', 'L0_ffn_ln_bias', 'L0_ffn_shared_in_w',
        'L0_ffn_shared_out_w', 'L0_ffn_shared_out_b', 'L0_ffn_expert_in_w', 'L0_ffn_expert_out_weight',
        'L0_ffn_expert_out_bias', 'L0_ffn_group_gate_w', 'L0_ffn_expert_gate_w', 'L0_ffn_group_bias',
        'L0_ffn_expert_bias']


def position_table():
    position = np.arange(HW, dtype=np.float32)[:, None]
    div_term = np.exp(np.arange(0, D, 2, dtype=np.float32) * np.float32(-np.log(10000.0) / D))
    table = np.zeros((HW, D), dtype=np.float32)
    table[:, 0::2] = np.sin(position * div_term)
    table[:, 1::2] = np.cos(position * div_term)
    return table


def kernel(**inputs):
    import concourse.bacc as bacc
    from concourse.bass_utils import run_bass_kernel_spmd

    nc = bacc.Bacc("TRN2", target_bir_lowering=False, num_devices=1)
    arrays, args = {}, []
    for name in _INS + ["pe_table"]:
        a = np.ascontiguousarray(inputs[name] if name in inputs else position_table())
        arrays[f"in_{name}_dram"] = a
        args.append(nc.dram_tensor(f"in_{name}_dram", a.shape, mybir.dt.from_np(a.dtype), kind="ExternalInput").ap())
    args.append(nc.dram_tensor("out_0_dram", (B, T, D), F32, kind="ExternalOutput").ap())
    fusion_kernel(nc, *args)
    r = run_bass_kernel_spmd(nc, [arrays], core_ids=[0])
    return r.results[0]["out_0_dram"]
```
